# Optimizing a Trainium2 kernel written in Bass

```python
import numpy as np
import jax
import jax.numpy as jnp

def _softmax(x, axis=-1):
    return jax.nn.softmax(x, axis=axis)

def _gelu(x):
    return jax.nn.gelu(x, approximate=True)

def _silu(x):
    return jax.nn.silu(x)

def _sigmoid(x):
    return jax.nn.sigmoid(x)

def _layernorm(x, axis=-1, eps=1e-05):
    m = jnp.mean(x, axis=axis, keepdims=True)
    v = jnp.var(x, axis=axis, keepdims=True)
    return (x - m) / jnp.sqrt(v + eps)

def _scatter_add(tgt, idx, src, axis=0):
    return tgt.at[idx].add(src)

def _segment_sum(src, seg, n):
    return jax.ops.segment_sum(src, seg, n)
kernel_name = 'mk_prb_d1_jaxref_r8_654f49'

def setup_inputs(seed: int=0):
    np.random.seed(seed)
    _w = jnp.asarray

    def _L0_attn_setup():
        import jax, jax.numpy as jnp
        import numpy as np
        import math
        B, T, E = (1, 256, 128)
        H = 8
        D = E // H // 2
        LAMBDA_INIT = 0.8 - 0.6 * math.exp(-0.3 * 1)
        SCALE_BASE = 512.0
        THETA = 10000.0

        def _rope_tables(T, d):
            inv_freq = 1.0 / THETA ** (jnp.arange(0, d, 2, dtype=jnp.float32) / d)
            pos = jnp.arange(T, dtype=jnp.float32)
            freqs = pos[:, None] * inv_freq[None, :]
            freqs = jnp.repeat(freqs, 2, axis=-1)
            sv = (jnp.arange(0, d, 2, dtype=jnp.float32) + 0.4 * d) / (1.4 * d)
            power = (pos - T // 2) / SCALE_BASE
            scale = sv[None, :] ** power[:, None]
            scale = jnp.concatenate([scale, scale], axis=-1)
            return (freqs, scale)

        def _rotate_half(x):
            x1 = x[..., 0::2]
            x2 = x[..., 1::2]
            return jnp.stack([-x2, x1], axis=-1).reshape(x.shape)

        def _apply_rope(t, freqs, scale):
            f = freqs[None, :, None, :]
            s = scale[None, :, None, :]
            return t * jnp.cos(f) * s + _rotate_half(t) * jnp.sin(f) * s
        key = jax.random.key(seed)
        ks = jax.random.split(key, 9)
        w = 0.02
        return {'x': jax.random.normal(ks[0], (B, T, E), dtype=jnp.float32), 'Wq': jax.random.normal(ks[1], (E, E), dtype=jnp.float32) * w, 'Wk': jax.random.normal(ks[2], (E, E), dtype=jnp.float32) * w, 'Wv': jax.random.normal(ks[3], (E, E), dtype=jnp.float32) * w, 'Wo': jax.random.normal(ks[4], (E, E), dtype=jnp.float32) * w, 'lambda_q1': jax.random.normal(ks[5], (D,), dtype=jnp.float32) * 0.1, 'lambda_k1': jax.random.normal(ks[6], (D,), dtype=jnp.float32) * 0.1, 'lambda_q2': jax.random.normal(ks[7], (D,), dtype=jnp.float32) * 0.1, 'lambda_k2': jax.random.normal(ks[8], (D,), dtype=jnp.float32) * 0.1}
    _L0_attn_in = _L0_attn_setup()

    def _L0_ffn_setup():
        import jax, jax.numpy as jnp
        import numpy as np
        D_MODEL = 128
        D_FF = 512
        N_ZONES = 8
        TOP_K = 3
        ROUTER_H = 32
        BATCH = 16
        SEQ = 256
        key = jax.random.key(seed)
        ks = jax.random.split(key, 8)
        s = lambda *dims: 1.0 / np.sqrt(dims[-2] if len(dims) > 1 else dims[-1])
        x = jax.random.normal(ks[0], (BATCH, SEQ, D_MODEL), dtype=jnp.float32)
        W1 = jax.random.normal(ks[1], (D_MODEL, ROUTER_H), dtype=jnp.float32) / np.sqrt(D_MODEL)
        b1 = jnp.zeros((ROUTER_H,), dtype=jnp.float32)
        W2 = jax.random.normal(ks[2], (ROUTER_H, N_ZONES), dtype=jnp.float32) / np.sqrt(ROUTER_H)
        b2 = jnp.zeros((N_ZONES,), dtype=jnp.float32)
        Wa = jax.random.normal(ks[3], (N_ZONES, D_MODEL, D_FF), dtype=jnp.float32) / np.sqrt(D_MODEL)
        Wb = jax.random.normal(ks[4], (N_ZONES, D_FF, D_MODEL), dtype=jnp.float32) / np.sqrt(D_FF)
        return {'x': x, 'W1': W1, 'b1': b1, 'W2': W2, 'b2': b2, 'Wa': Wa, 'Wb': Wb}
    _L0_ffn_in = _L0_ffn_setup()
    _d = {'L0_attn_x': _L0_attn_in['x'], 'L0_attn_Wq': _L0_attn_in['Wq'], 'L0_attn_Wk': _L0_attn_in['Wk'], 'L0_attn_Wv': _L0_attn_in['Wv'], 'L0_attn_Wo': _L0_attn_in['Wo'], 'L0_attn_lambda_q1': _L0_attn_in['lambda_q1'], 'L0_attn_lambda_k1': _L0_attn_in['lambda_k1'], 'L0_attn_lambda_q2': _L0_attn_in['lambda_q2'], 'L0_attn_lambda_k2': _L0_attn_in['lambda_k2'], 'L0_ffn_W1': _L0_ffn_in['W1'], 'L0_ffn_b1': _L0_ffn_in['b1'], 'L0_ffn_W2': _L0_ffn_in['W2'], 'L0_ffn_b2': _L0_ffn_in['b2'], 'L0_ffn_Wa': _L0_ffn_in['Wa'], 'L0_ffn_Wb': _L0_ffn_in['Wb']}
    _x0 = _d['L0_attn_x']
    _d['L0_attn_x'] = jax.random.normal(jax.random.fold_in(jax.random.key(seed), 1), (2, 1024, 128), dtype=_x0.dtype)
    del _x0
    return _d

def reference(L0_attn_x, L0_attn_Wq, L0_attn_Wk, L0_attn_Wv, L0_attn_Wo, L0_attn_lambda_q1, L0_attn_lambda_k1, L0_attn_lambda_q2, L0_attn_lambda_k2, L0_ffn_W1, L0_ffn_b1, L0_ffn_W2, L0_ffn_b2, L0_ffn_Wa, L0_ffn_Wb):

    def _L0_attn_ref(x, Wq, Wk, Wv, Wo, lambda_q1, lambda_k1, lambda_q2, lambda_k2):
        import jax, jax.numpy as jnp
        import numpy as np
        import math
        B, T, E = (1, 256, 128)
        H = 8
        D = E // H // 2
        LAMBDA_INIT = 0.8 - 0.6 * math.exp(-0.3 * 1)
        SCALE_BASE = 512.0
        THETA = 10000.0

        def _rope_tables(T, d):
            inv_freq = 1.0 / THETA ** (jnp.arange(0, d, 2, dtype=jnp.float32) / d)
            pos = jnp.arange(T, dtype=jnp.float32)
            freqs = pos[:, None] * inv_freq[None, :]
            freqs = jnp.repeat(freqs, 2, axis=-1)
            sv = (jnp.arange(0, d, 2, dtype=jnp.float32) + 0.4 * d) / (1.4 * d)
            power = (pos - T // 2) / SCALE_BASE
            scale = sv[None, :] ** power[:, None]
            scale = jnp.concatenate([scale, scale], axis=-1)
            return (freqs, scale)

        def _rotate_half(x):
            x1 = x[..., 0::2]
            x2 = x[..., 1::2]
            return jnp.stack([-x2, x1], axis=-1).reshape(x.shape)

        def _apply_rope(t, freqs, scale):
            f = freqs[None, :, None, :]
            s = scale[None, :, None, :]
            return t * jnp.cos(f) * s + _rotate_half(t) * jnp.sin(f) * s
        b, t, e = x.shape
        scaling = D ** (-0.5)
        q = (x @ Wq.T).reshape(b, t, 2 * H, D)
        k = (x @ Wk.T).reshape(b, t, 2 * H, D)
        v = (x @ Wv.T).reshape(b, t, H, 2 * D)
        freqs, scale = _rope_tables(t, D)
        q = _apply_rope(q, freqs, scale)
        k = _apply_rope(k, freqs, 1.0 / scale)
        q = jnp.transpose(q, (0, 2, 1, 3)) * scaling
        k = jnp.transpose(k, (0, 2, 1, 3))
        v = jnp.transpose(v, (0, 2, 1, 3))
        scores = jnp.einsum('bhtd,bhsd->bhts', q, k)
        probs = jax.nn.softmax(scores.astype(jnp.float32), axis=-1).astype(scores.dtype)
        lam1 = jnp.exp(jnp.sum(lambda_q1 * lambda_k1))
        lam2 = jnp.exp(jnp.sum(lambda_q2 * lambda_k2))
        lam = lam1 - lam2 + LAMBDA_INIT
        probs = probs.reshape(b, H, 2, t, t)
        diff = probs[:, :, 0] - lam * probs[:, :, 1]
        attn = jnp.einsum('bhts,bhsd->bhtd', diff, v)
        attn = attn * jax.lax.rsqrt(jnp.mean(attn * attn, axis=-1, keepdims=True) + 1e-05)
        attn = attn * (1.0 - LAMBDA_INIT)
        attn = jnp.transpose(attn, (0, 2, 1, 3)).reshape(b, t, e)
        return attn @ Wo.T

    def _L0_ffn_ref(x, W1, b1, W2, b2, Wa, Wb):
        import jax, jax.numpy as jnp
        import numpy as np
        D_MODEL = 128
        D_FF = 512
        N_ZONES = 8
        TOP_K = 3
        ROUTER_H = 32
        BATCH = 16
        SEQ = 256
        pooled = x.mean(axis=1)
        h = jnp.tanh(pooled @ W1 + b1)
        logits = h @ W2 + b2
        probs = jax.nn.softmax(logits, axis=-1)
        top_p, top_i = jax.lax.top_k(probs, TOP_K)
        top_w = top_p / top_p.sum(axis=-1, keepdims=True)
        onehot = jax.nn.one_hot(top_i, N_ZONES, dtype=x.dtype)
        w = jnp.einsum('bk,bke->be', top_w, onehot)
        zone_outputs = jnp.zeros_like(x)
        for e in range(N_ZONES):
            z = jax.nn.gelu(x @ Wa[e]) @ Wb[e]
            zone_outputs = zone_outputs + z * w[:, e, None, None]
        return x + zone_outputs
    x = L0_attn_x
    xn = _layernorm(x, axis=-1)
    x = x + _L0_attn_ref(xn, L0_attn_Wq, L0_attn_Wk, L0_attn_Wv, L0_attn_Wo, L0_attn_lambda_q1, L0_attn_lambda_k1, L0_attn_lambda_q2, L0_attn_lambda_k2) + _L0_ffn_ref(xn, L0_ffn_W1, L0_ffn_b1, L0_ffn_W2, L0_ffn_b2, L0_ffn_Wa, L0_ffn_Wb)
    return x

_drawn_inputs = setup_inputs


def setup_inputs(seed=0):
    import zlib

    import numpy as np

    out = dict(_drawn_inputs(seed))
    spreads = {'L0_ffn_b1': (0.0, 0.1), 'L0_ffn_b2': (0.0, 0.8)}
    factors = {'L0_attn_Wq': 4.641,
     'L0_attn_Wk': 4.382,
     'L0_attn_lambda_q1': 174.59,
     'L0_attn_lambda_k1': 8.0,
     'L0_attn_lambda_q2': 64.0,
     'L0_attn_lambda_k2': 64.0,
     'L0_ffn_W1': 8.0}
    for name, (base, spread) in spreads.items():
        noise = np.random.default_rng([zlib.crc32(name.encode()), seed]).standard_normal(out[name].shape)
        drawn = base * np.exp(spread * noise) if base else spread * noise
        out[name] = jnp.asarray(drawn.astype(out[name].dtype))
    for name, factor in factors.items():
        out[name] = (out[name] * factor).astype(out[name].dtype)
    return out
```

```python
from contextlib import ExitStack
import math

import numpy as np

import concourse.bass as bass
from concourse import mybir

ALU = mybir.AluOpType
ACT = mybir.ActivationFunctionType
F32 = mybir.dt.float32
F32R = mybir.dt.float32r
AX = mybir.AxisListType

P = 128
BATCH, SEQ = 2, 1024
TOKENS = BATCH * SEQ
TILES = TOKENS // P
TB = SEQ // P
BANK = 512
CHUNKS = TOKENS // BANK
CB = SEQ // BANK
HEADS, SUBHEADS, DQ, DV = 8, 16, 8, 16
LAMBDA_INIT = 0.8 - 0.6 * math.exp(-0.3)
EPS = 1e-5
LAMBDA_RANGE = 2.0 ** 46
SQRT_LEAST = 2.0 ** -110
FLT_MAX = float(np.finfo(np.float32).max)
QUAD = 32
GJ = P // QUAD
GB = SUBHEADS // GJ
GROUPS = BATCH * GB
PROD_ROWS = 3 * DQ
MAX_ROW = PROD_ROWS
ZONES, TOP_K, FF, ROUTER = 8, 3, 512, 32
FC = FF // P
UZ = CHUNKS * FC // 2
UNITS = ZONES * UZ
H_BUFS = 4
STEPS = SEQ // BANK * TB
ALL_STEPS = GROUPS * STEPS
UG = TB * GJ
ALL_UNITS = GROUPS * UG
LEAD = 26
BACK = (20, 22, 24, 25)
PAIR = 2 * STEPS
PAIRS = GROUPS // 2

ARENA = 206 * 1024

C_ID, C_BLK, C_E0, C_E1, C_SEL, C_TRI, C_ONE, C_END = 0, 128, 256, 288, 320, 576, 640, 768

B_MAX, B_PV, B_MISC = 4, 6, 7


def build(nc, x, wqkv, wo, lam, w1, b1, w2, b2, wa, wb, consts, tables, out):
    with ExitStack() as ctx:
        def sem(name):
            return ctx.enter_context(nc.semaphore(name))

        ps = ctx.enter_context(nc.psum_tensor("ps", [P, 8, BANK], F32))

        base = (nc.sbuf_base + 31) // 32 * 32
        ctx.enter_context(nc.sbuf_tensor("arena", [P, ARENA // 4], F32))

        def region(start, *parts):
            at, made = start, []
            for name, shape, dt in parts:
                made.append(nc.alloc_sbuf_tensor_at(name, shape, dt, offset=base + at))
                at += (4 * math.prod(shape[1:]) + 31) // 32 * 32
            return made, at

        (X, cst, wo_in, identR, XN, V1, xnH, xnL, Q, lam_in, w1_in, b1_in, w2_in, b2_in, eps, stats, mv, rstd,
         pooled, hid, rt, wbc, lam_p, lam_e, lt, epsc, limit, lnt, comb, part_max, neg_max, maxH, maxL, maxones), r1 = region(
            0,
            ("X", [P, TILES, P], F32), ("cst", [P, C_END], F32), ("wo_in", [P, P], F32),
            ("identR", [P, P], F32R), ("XN", [P, TILES, P], F32),
            ("V", [P, GROUPS * TB * 2 * QUAD], F32),
            ("xnH", [P, TOKENS], F32R), ("xnL", [P, TOKENS], F32R),
            ("Q", [P, 2, SEQ], F32R),
            ("lam_in", [DQ, 4], F32), ("w1_in", [P, ROUTER], F32), ("b1_in", [ROUTER, 1], F32),
            ("w2_in", [ROUTER, ZONES], F32), ("b2_in", [1, ZONES], F32), ("eps", [P, 1], F32),
            ("stats", [P, TILES, 6], F32), ("mv", [P, TILES, 2], F32), ("rstd", [P, TILES], F32),
            ("pooled", [P, BATCH], F32), ("hid", [ROUTER, BATCH], F32), ("rt", [BATCH, 256], F32),
            ("wbc", [P, BATCH * ZONES], F32), ("lam_p", [DQ, 2], F32), ("lam_e", [P, 2], F32),
            ("lt", [P, 8], F32), ("epsc", [P, 1], F32), ("limit", [P, 1], F32), ("lnt", [P, 2, TB], F32), ("comb", [P, QUAD], F32),
            ("part_max", [P, 2, 16, 2], F32), ("neg_max", [P, 2, 16], F32),
            ("maxH", [16, 2, P], F32R), ("maxL", [16, 2, P], F32R),
            ("maxones", [2, SEQ], F32R))
        (tab, rot, rope), r2a = region(
            r1,
            ("tab", [P, 4, SEQ], F32),
            ("rot", [P, 2, 2, BANK], F32),
            ("rope", [P, 2, BANK], F32))
        (K,), r2 = region(r1, ("K", [P, 2, GJ, SEQ], F32R))
        (ropeH, ropeL, w_in, wH, wL), r3 = region(
            r2, ("ropeH", [P, 2, SEQ], F32R), ("ropeL", [P, 2, SEQ], F32R),
            ("w_in", [P, 5, P], F32), ("wH", [P, 5, P], F32R), ("wL", [P, 5, P], F32R))
        (zT, Vg), r3b = region(
            r2, ("zT", [P, TOKENS], F32), ("Vg", [P, 2, TB, 2, QUAD], F32))
        (wa_raw, wb_raw, waH, waL, wbH, wbL, h, hH, hL), r4 = region(
            r3, ("wa_raw", [P, 2, FF], F32), ("wb_raw", [P, 2, FF], F32),
            ("waH", [P, 2, FF], F32R), ("waL", [P, 2, FF], F32R),
            ("wbH", [P, 2, BATCH, FF], F32R), ("wbL", [P, 2, BATCH, FF], F32R),
            ("h", [P, 2, 2 * BANK], F32),
            ("hH", [P, H_BUFS, 2 * BANK], F32R), ("hL", [P, H_BUFS, 2 * BANK], F32R))
        (E, A, den, rden, U), r4b = region(
            r3, ("E", [P, 2, GJ, BANK], F32), ("A", [P, 2, BANK], F32), ("den", [P, 2, BANK], F32),
            ("rden", [P, 2, BANK], F32), ("U", [P, 2 * GROUPS * BANK], F32))
        assert r2a <= r2 and r3b <= r3 and max(r4, r4b) <= ARENA, (ARENA, r1, r2, r3, r4, r4b)
        V = V1[:].rearrange("p (g t h d) -> p g t h d", g=GROUPS, t=TB, h=2)
        ident = cst[:, C_ID:C_ID + P]
        blocksum = cst[:, C_BLK:C_BLK + P]
        ones = cst[:, C_ONE:C_ONE + P]
        RES = XN
        at, sq, sd, rms = (E[:, 0, k, :] for k in range(GJ))
        an = [zT[:, k * BANK:(k + 1) * BANK] for k in range(2)]

        k_scr = nc.dram_tensor("k_scr", (GROUPS, GJ, PROD_ROWS, SEQ), F32, kind="Internal").ap()
        q_scr = nc.dram_tensor("q_scr", (GROUPS, P, SEQ), F32, kind="Internal").ap()

        x_in = [sem(f"x_in{b}") for b in range(BATCH)]
        c_in, w_arr, s_in, tab_in = sem("c_in"), sem("w_arr"), sem("s_in"), sem("tab_in")
        raw_in = [sem(f"raw_in{i}") for i in range(2)]
        scr_out, zero_out, ones_in, kq_in, qmax_in, out_done = (
            sem("scr_out"), sem("zero_out"), sem("ones_in"), sem("kq_in"), sem("qmax_in"), sem("out_done"))
        sp_waited, pool_waited, dve_waited = sem("sp_waited"), sem("pool_waited"), sem("dve_waited")
        fills, fills2 = sem("fills"), sem("fills2")
        mv_done, sd_done, rstd_done, xn_done = sem("mv_done"), sem("sd_done"), sem("rstd_done"), sem("xn_done")
        xt_done, xh_done, xl_done, id_done = sem("xt_done"), sem("xh_done"), sem("xl_done"), sem("id_done")
        wh_done, w_split = sem("wh_done"), sem("w_split")
        proj_done, rot_done, rope_done, ropeh_done, ropel_done = (
            sem("proj_done"), sem("rot_done"), sem("rope_done"), sem("ropeh_done"), sem("ropel_done"))
        v_done, v_out = sem("v_done"), sem("v_out")
        pool_ps, pool_sb, hid_ps, hid_sb, logit_ps, negl, expl, wsel, wb_ps, wbc_done = (
            sem("pool_ps"), sem("pool_sb"), sem("hid_ps"), sem("hid_sb"), sem("logit_ps"),
            sem("negl"), sem("expl"), sem("wsel"), sem("wb_ps"), sem("wbc_done"))
        lam_prod, lam_ps, lam_exp, comb_done = sem("lam_prod"), sem("lam_ps"), sem("lam_exp"), sem("comb_done")
        dch = sem("dch")
        wah_done, wa_split, wbh_done, wb_split = sem("wah_done"), sem("wa_split"), sem("wbh_done"), sem("wb_split")
        g1_done, gelu_done, hh_done, split_done, hs_free, z_out, zt_done, res_done = (
            sem("g1_done"), sem("gelu_done"), sem("hh_done"), sem("split_done"), sem("hs_free"),
            sem("z_out"), sem("zt_done"), sem("res_done"))
        max_done, red_done, neg_done, negt_done, maxh_done, maxl_done = (
            sem("max_done"), sem("red_done"), sem("neg_done"), sem("negt_done"), sem("maxh_done"), sem("maxl_done"))
        st_done, exp_done, e_free, vg_done, a_out, den_done, rden_done, u_free = (
            sem("st_done"), sem("exp_done"), sem("e_free"), sem("vg_done"),
            sem("a_out"), sem("den_done"), sem("rden_done"), sem("u_free"))
        at_ps, at_out, sq_done, ms_ps, std_done, rms_done, an_done, o_ps, o_done = (
            sem("at_ps"), sem("at_out"), sem("sq_done"), sem("ms_ps"), sem("std_done"), sem("rms_done"),
            sem("an_done"), sem("o_ps"), sem("o_done"))

        block = ctx.enter_context(nc.Block())

        @block.sync
        def _(sp):
            for b in range(BATCH):
                sp.dma_start(X[:, b * TB:(b + 1) * TB, :],
                             x[b * SEQ:(b + 1) * SEQ, :].rearrange("(n p) d -> p n d", p=P)).then_inc(x_in[b], 16)
            sp.dma_start(w_in[:], wqkv).then_inc(w_arr, 16)

            def raw_load(e, par):
                sp.sem_inc(sp_waited, 1)
                sp.dma_start(wa_raw[:, par, :], wa[e]).then_inc(raw_in[par], 16)
                sp.dma_start(wb_raw[:, par, :], wb[e]).then_inc(raw_in[par], 16)

            raw_load(0, 0)
            raw_load(1, 1)
            sp.wait_ge(fills2, 1)
            for half in range(2):
                sp.dma_start(q_scr[half * GB:(half + 1) * GB].rearrange("g (j s r) t -> (g j) s r t", j=GJ, r=DQ)[:, 3],
                             ropeL[:, 1, :].bitcast(F32)).then_inc(zero_out, 16)
            for n in range(2 * BATCH):
                b, kind = n // 2, n % 2
                sp.wait_ge(ropel_done, CB * (n + 1))
                for part, places in ((ropeH, ((0, 1), (0, 2))[kind]), (ropeL, ((2,), (1,))[kind])):
                    for s in places:
                        if kind:
                            dst = k_scr[b * GB:(b + 1) * GB].rearrange("g j (s r) t -> (g j) s r t", r=DQ)[:, s]
                        else:
                            dst = q_scr[b * GB:(b + 1) * GB].rearrange("g (j s r) t -> (g j) s r t", j=GJ, r=DQ)[:, s]
                        sp.dma_start(dst, part[:, n % 2, :].bitcast(F32)).then_inc(scr_out, 16)
                sp.wait_ge(scr_out, 48 * (n + 1))
            sp.wait_ge(zero_out, 32)
            sp.wait_ge(fills, 3)
            for par in range(2):
                for j in range(GJ):
                    r = QUAD * j + MAX_ROW
                    sp.dma_start(K[r:r + 2, par, j, :].bitcast(F32), maxones[0:2, :].bitcast(F32)).then_inc(ones_in, 16)

            def kq_load(i, par):
                sp.sem_inc(sp_waited, 1)
                for j in range(GJ):
                    sp.dma_start(K[QUAD * j:QUAD * j + PROD_ROWS, par, j, :].bitcast(F32), k_scr[i, j]).then_inc(kq_in, 16)
                sp.dma_start(Q[:, par, :].bitcast(F32), q_scr[i]).then_inc(kq_in, 16)

            sp.wait_ge(ones_in, 16 * 2 * GJ)
            kq_load(0, 0)
            sp.wait_ge(kq_in, 16 * (GJ + 1))
            kq_load(1, 1)
            with sp.Fori(0, ZONES // 2 - 1) as it:
                for par in range(2):
                    sp.wait_ge(wa_split, 2 * it + par + 1)
                    sp.wait_ge(wb_split, 2 * it + par + 1)
                    raw_load(2 * it + par + 2, par)
            sp.wait_ge(kq_in, 2 * 16 * (GJ + 1))

            def max_rows(i, par, half):
                sp.wait_ge(maxl_done, 2 * i + half + 1)
                for part, row in ((maxH, MAX_ROW), (maxL, MAX_ROW + 1)):
                    dst = Q[row:P:QUAD, par, half * BANK:(half + 1) * BANK].bitcast(F32)
                    sp.dma_start(dst.rearrange("j (t c) -> j t c", c=P), part[:, half, :].bitcast(F32)).then_inc(qmax_in, 16)
                sp.wait_ge(qmax_in, 32 * (2 * i + half + 1))
                sp.sem_inc(sp_waited, 1)

            max_rows(0, 0, 0)

            def turn(it, last):
                for p in range(2):
                    i = 2 * it + p
                    max_rows(i, p, 1)
                    if not (last and p):
                        max_rows(i + 1, 1 - p, 0)
                    if not last:
                        sp.wait_ge(st_done, 2 * STEPS * (i + 1))
                        kq_load(i + 2, p)
                        sp.wait_ge(kq_in, 16 * (GJ + 1) * (i + 3))
                        sp.sem_inc(sp_waited, 1)

            with sp.Fori(0, PAIRS - 1) as it:
                turn(it, False)
            turn(PAIRS - 1, True)
            for c in range(CHUNKS):
                sp.wait_ge(o_done, c + 1)
                sp.dma_start(out[c * BANK:(c + 1) * BANK, :].rearrange("(n p) d -> p n d", p=P),
                             RES[:, c * FC:(c + 1) * FC, :]).then_inc(out_done, 16)
            sp.wait_ge(out_done, 16 * CHUNKS)

        @block.gpsimd
        def _(pool):
            nc.gpsimd.memset(eps[:], EPS).then_inc(fills, 1)
            nc.gpsimd.memset(ropeL[:, 1, :].bitcast(F32), 0.0).then_inc(fills2, 1)
            nc.gpsimd.memset(V1[:], 1.0).then_inc(fills2, 1)
            pool.wait_ge(w_arr, 16)
            nc.gpsimd.tensor_copy(wH[:], w_in[:]).then_inc(wh_done, 1)
            pool.wait_ge(wh_done, 1)
            nc.gpsimd.tensor_tensor(wL[:], w_in[:], wH[:], ALU.subtract).then_inc(w_split, 1)

            def wa_zone(e, par, first):
                pool.wait_ge(raw_in[par], 32 * (e // 2 + 1) if first else 32 * (e + 1))
                if not first:
                    pool.wait_ge(g1_done, UZ * (2 * e + par - 1))
                    pool.sem_inc(pool_waited, 1)
                nc.gpsimd.tensor_copy(waH[:, par, :], wa_raw[:, par, :]).then_inc(wah_done, 1)
                pool.wait_ge(wah_done, e + 1 if first else 2 * e + par + 1)
                nc.gpsimd.tensor_tensor(waL[:, par, :], wa_raw[:, par, :], waH[:, par, :],
                                        ALU.subtract).then_inc(wa_split, 1)

            for m in range(2 * BATCH * CB):
                n, c = m // CB, m % CB
                pool.wait_ge(rot_done, 2 * (m + 1))
                if m >= 2:
                    pool.wait_ge(ropel_done, m - 1)
                nc.gpsimd.tensor_tensor(rope[:, m % 2, :], rot[:, m % 2, 0, :], rot[:, m % 2, 1, :],
                                        ALU.add).then_inc(rope_done, 1)
                pool.wait_ge(rope_done, m + 1)
                if n == 1 and c == 0:
                    pool.wait_ge(zero_out, 32)
                if n >= 2:
                    pool.wait_ge(scr_out, 48 * (n - 1))
                nc.gpsimd.tensor_copy(ropeH[:, n % 2, c * BANK:(c + 1) * BANK],
                                      rope[:, m % 2, :]).then_inc(ropeh_done, 1)
                pool.wait_ge(ropeh_done, m + 1)
                nc.gpsimd.tensor_tensor(ropeL[:, n % 2, c * BANK:(c + 1) * BANK], rope[:, m % 2, :],
                                        ropeH[:, n % 2, c * BANK:(c + 1) * BANK],
                                        ALU.subtract).then_inc(ropel_done, 1)
                if m == 3:
                    wa_zone(0, 0, True)
            pool.wait_ge(ropel_done, 2 * BATCH * CB)
            nc.gpsimd.memset(K[:].bitcast(F32), 0.0).then_inc(fills, 1)
            nc.gpsimd.memset(maxones[:].bitcast(F32), 1.0).then_inc(fills, 1)
            wa_zone(1, 1, True)
            with pool.Fori(1, ZONES // 2) as e2:
                for par in range(2):
                    wa_zone(e2, par, False)

            pool.wait_ge(scr_out, 48 * 2 * BATCH)
            def v_group(i, par):
                pool.sem_inc(pool_waited, 1)
                nc.gpsimd.tensor_copy(Vg[:, par].rearrange("p a h d -> p (a h d)"),
                                      V1[:, bass.ts(i, TB * 2 * QUAD)]).then_inc(vg_done, 1)

            pool.wait_ge(v_out, CHUNKS)
            v_group(0, 0)
            v_group(1, 1)

            def turn(it, last):
                for p in range(2):
                    i = 2 * it + p
                    for th in range(2):
                        a = 2 * i + th
                        pool.wait_ge(rden_done, a + 1)
                        nc.gpsimd.tensor_tensor(U[:, bass.ts(a, BANK)], A[:, th, :], rden[:, th, :],
                                                ALU.mult).then_inc(u_free, 1)
                    if not last:
                        pool.wait_ge(e_free, 2 + STEPS * (i + 1))
                        v_group(i + 2, p)

            pool.sem_inc(u_free, 2)
            with pool.Fori(0, PAIRS - 1) as it:
                turn(it, False)
            turn(PAIRS - 1, True)

        @block.scalar
        def _(act):
            act.dma_start(cst[:], consts).then_inc(c_in, 16)
            for dst, src in ((w1_in, w1), (b1_in, b1), (w2_in, w2), (b2_in, b2), (lam_in, lam)):
                act.dma_start(dst[:], src).then_inc(s_in, 16)
            act.dma_start(tab[:], tables).then_inc(tab_in, 16)
            act.dma_start(wo_in[:], wo).then_inc(s_in, 16)
            act.wait_ge(fills, 1)
            for b in range(BATCH):
                act.wait_ge(mv_done, TB * (b + 1))
                nc.scalar.activation(rstd[:, b * TB:(b + 1) * TB], mv[:, b * TB:(b + 1) * TB, 1], ACT.Sqrt,
                                     bias=eps[:, 0:1]).then_inc(sd_done, 1)
            act.wait_ge(c_in, 16)
            nc.scalar.activation(identR[:], ident, ACT.Copy).then_inc(id_done, 1)
            for c in range(CHUNKS):
                act.wait_ge(xt_done, c + 1)
                nc.scalar.activation(xnH[:, c * BANK:(c + 1) * BANK], ps[:, c, :], ACT.Copy).then_inc(xh_done, 1)
            act.wait_ge(pool_ps, 1)
            nc.scalar.activation(pooled[:], ps[:, 7, 0:BATCH], ACT.Copy, scale=1.0 / SEQ).then_inc(pool_sb, 1)
            act.wait_ge(hid_ps, 1)
            act.wait_ge(s_in, 16 * 6)
            nc.scalar.activation(hid[:], ps[0:ROUTER, 7, 8:8 + BATCH], ACT.Tanh, bias=b1_in[:, 0:1]).then_inc(hid_sb, 1)
            act.wait_ge(lam_ps, 1)
            nc.scalar.activation(lam_e[:], ps[:, 7, 32:34], ACT.Exp).then_inc(lam_exp, 1)
            act.wait_ge(negl, 1)
            nc.scalar.activation(rt[:, 8:16], ps[0:BATCH, 7, 16:16 + ZONES], ACT.Exp, bias=rt[:, 0:1]).then_inc(expl, 1)
            act.wait_ge(fills2, 2)
            for c in range(CHUNKS):
                act.wait_ge(v_done, c + 1)
                b = c // CB
                for k in range(FC):
                    st = (c % CB) * FC + k
                    last = nc.scalar.activation(
                        V[:, b * GB:(b + 1) * GB, st, :, 0:DV],
                        ps[:, c, k * P:(k + 1) * P].rearrange("p (g h d) -> p g h d", g=GB, h=2), ACT.Copy)
                last.then_inc(v_out, 1)

            def gelu(n, buf):
                act.wait_ge(g1_done, n + 1)
                nc.scalar.activation(h[:, buf, :], ps[:, 4 + 2 * buf:6 + 2 * buf, :].rearrange("p a n -> p (a n)"),
                                     ACT.Gelu_apprx_tanh).then_inc(gelu_done, 1)

            gelu(0, 0)
            gelu(1, 1)

            def gelu_turn(it, last):
                for s in range(2 * UZ - 2 * last):
                    act.wait_ge(split_done, 2 * UZ * it + s + 1)
                    gelu(2 * UZ * it + s + 2, s % 2)

            with act.Fori(0, ZONES // 2 - 1) as it:
                gelu_turn(it, False)
            gelu_turn(ZONES // 2 - 1, True)
            act.wait_ge(hs_free, H_BUFS + UNITS)
            for c in range(CHUNKS):
                nc.scalar.activation(zT[:, c * BANK:(c + 1) * BANK], ps[:, c, :], ACT.Copy).then_inc(z_out, 1)

            def turn(it, last):
                for s in range(PAIR):
                    n = PAIR * it + s
                    for jj in range(2):
                        act.wait_ge(st_done, 2 * n + jj + 1)
                        act.wait_ge(e_free, n + 1)
                        nc.scalar.activation(
                            E[:, s % 2, 2 * jj:2 * jj + 2, :].rearrange("p j t -> p (j t)"),
                            ps[:, 2 * jj:2 * jj + 2, :].rearrange("p j t -> p (j t)"), ACT.Exp).then_inc(exp_done, 1)
                    if s % TB == 0 and s > 0:
                        evacuate(PAIR // TB * it + s // TB - 1, (s // TB - 1) % 2)
                evacuate(PAIR // TB * it + PAIR // TB - 1, 1)

            def evacuate(a, th):
                act.wait_ge(e_free, 2 + TB * (a + 1))
                act.wait_ge(u_free, a + 1)
                nc.scalar.activation(A[:, th, :], ps[:, B_PV, :], ACT.Copy).then_inc(a_out, 1)

            with act.Fori(0, PAIRS - 1) as it:
                turn(it, False)
            turn(PAIRS - 1, True)

            for c in range(CHUNKS):
                act.wait_ge(at_ps, c + 1)
                if c:
                    act.wait_ge(an_done, c)
                nc.scalar.activation(at, ps[:, c % 2, :], ACT.Copy).then_inc(at_out, 1)
                nc.scalar.activation(sq, ps[:, c % 2, :], ACT.Square).then_inc(sq_done, 1)
                act.wait_ge(ms_ps, c + 1)
                nc.scalar.activation(sd, ps[:, 2 + c % 2, :], ACT.Sqrt, scale=1.0 / DV, bias=epsc[:, 0:1]).then_inc(std_done, 1)

        @block.vector
        def _(dve):
            chain = [0]

            def link(ins):
                chain[0] += 1
                ins.then_inc(dch, 1)
                dve.wait_ge(dch, chain[0])

            for b in range(BATCH):
                dve.wait_ge(x_in[b], 16)
                for n in range(b * TB, (b + 1) * TB):
                    last = nc.vector.bn_stats(stats[:, n, :], X[:, n, :])
                link(last)
                for n in range(b * TB, (b + 1) * TB):
                    nc.vector.bn_aggr(mv[:, n, :], stats[:, n, :]).then_inc(mv_done, 1)
            for b in range(BATCH):
                r, v, t = rstd[:, b * TB:(b + 1) * TB], lnt[:, 0, :], lnt[:, 1, :]
                dve.wait_ge(sd_done, b + 1)
                link(nc.vector.reciprocal(r, r))
                link(nc.vector.tensor_scalar(v, mv[:, b * TB:(b + 1) * TB, 1], EPS, -0.5, ALU.add, ALU.mult))
                link(nc.vector.tensor_tensor(t, r, r, ALU.mult))
                link(nc.vector.tensor_tensor(t, t, v, ALU.mult))
                link(nc.vector.scalar_tensor_tensor(r, t, 1.5, r, ALU.add, ALU.mult))
                for n in range(b * TB, (b + 1) * TB):
                    nc.vector.tensor_scalar(XN[:, n, :], X[:, n, :], mv[:, n, 0:1], rstd[:, n:n + 1],
                                            ALU.subtract, ALU.mult).then_inc(xn_done, 1)
            dve.wait_ge(s_in, 16 * 6)
            nc.vector.tensor_tensor(lam_p[:], lam_in[:, 0:4:2], lam_in[:, 1:4:2], ALU.mult).then_inc(lam_prod, 1)
            for c in range(CHUNKS):
                dve.wait_ge(xh_done, c + 1)
                nc.vector.tensor_tensor(xnL[:, c * BANK:(c + 1) * BANK], ps[:, c, :],
                                        xnH[:, c * BANK:(c + 1) * BANK], ALU.subtract).then_inc(xl_done, 1)

            dve.wait_ge(tab_in, 16)

            def rotary(m):
                kind, c = (m // CB) % 2, m % CB
                for r in range(2):
                    k = 2 * m + r
                    dve.wait_ge(proj_done, k + 1)
                    if m >= 2:
                        dve.wait_ge(rope_done, m - 1)
                    nc.vector.tensor_tensor(rot[:, m % 2, r, :], ps[:, 4 + k % 3, :],
                                            tab[:, 2 * kind + r, c * BANK:(c + 1) * BANK],
                                            ALU.mult).then_inc(rot_done, 1)

            for m in range(4):
                rotary(m)

            dve.wait_ge(logit_ps, 1)
            nc.vector.tensor_reduce(rt[:, 0:1], ps[0:BATCH, 7, 16:16 + ZONES], AX.X, ALU.max,
                                    negate=True).then_inc(negl, 1)
            for m in range(4, 6):
                rotary(m)
            dve.wait_ge(expl, 1)
            e_, p_ = rt[:, 8:16], rt[:, 16:24]
            gt = rt[:, 64:128].rearrange("b (e j) -> b e j", j=ZONES)
            eq = rt[:, 128:192].rearrange("b (e j) -> b e j", j=ZONES)
            tri = cst[0:BATCH, C_TRI:C_TRI + 64].rearrange("b (e j) -> b e j", j=ZONES)
            pj = rt[:, 16:24].unsqueeze(1).broadcast_to([BATCH, ZONES, ZONES])
            pe_ = rt[:, 16:24].unsqueeze(2).broadcast_to([BATCH, ZONES, ZONES])
            link(nc.vector.tensor_reduce(rt[:, 1:2], e_, AX.X, ALU.add))
            link(nc.vector.reciprocal(rt[:, 2:3], rt[:, 1:2]))
            link(nc.vector.tensor_scalar(p_, e_, rt[:, 2:3], None, ALU.mult))
            link(nc.vector.tensor_tensor(gt, pj, pe_, ALU.is_gt))
            link(nc.vector.tensor_tensor(eq, pj, pe_, ALU.is_equal))
            link(nc.vector.tensor_tensor(eq, eq, tri, ALU.mult))
            link(nc.vector.tensor_tensor(gt, gt, eq, ALU.add))
            link(nc.vector.tensor_reduce(rt[:, 24:32], gt, AX.X, ALU.add))
            link(nc.vector.tensor_scalar(rt[:, 32:40], rt[:, 24:32], TOP_K - 0.5, None, ALU.is_lt))
            link(nc.vector.tensor_tensor(rt[:, 40:48], rt[:, 32:40], p_, ALU.mult))
            link(nc.vector.tensor_reduce(rt[:, 3:4], rt[:, 40:48], AX.X, ALU.add))
            link(nc.vector.reciprocal(rt[:, 4:5], rt[:, 3:4]))
            nc.vector.tensor_scalar(rt[:, 48:56], rt[:, 40:48], rt[:, 4:5], None, ALU.mult).then_inc(wsel, 1)
            for m in range(6, 8):
                rotary(m)
            dve.wait_ge(lam_exp, 1)
            nl, ab, cc, c2, nlc = (lt[:, k:k + 1] for k in range(5))
            link(nc.vector.scalar_tensor_tensor(nl, lam_e[:, 1:2], LAMBDA_INIT, lam_e[:, 0:1],
                                                ALU.subtract, ALU.subtract))
            link(nc.vector.tensor_scalar(ab, nl, -1.0, None, ALU.mult))
            link(nc.vector.tensor_tensor(ab, ab, nl, ALU.max))
            link(nc.vector.tensor_scalar(ab, ab, 1.0, None, ALU.add))
            link(nc.vector.reciprocal(cc, ab))
            link(nc.vector.tensor_scalar(cc, cc, LAMBDA_RANGE, 1.0, ALU.mult, ALU.min))
            link(nc.vector.tensor_tensor(c2, cc, cc, ALU.mult))
            link(nc.vector.tensor_scalar(epsc[:], c2, EPS, SQRT_LEAST, ALU.mult, ALU.max))
            link(nc.vector.tensor_scalar(limit[:], c2, FLT_MAX, None, ALU.mult))
            link(nc.vector.tensor_tensor(nlc, nl, cc, ALU.mult))
            link(nc.vector.tensor_scalar(comb[:], cst[:, C_E0:C_E0 + QUAD], cc, None, ALU.mult))
            nc.vector.scalar_tensor_tensor(comb[:], cst[:, C_E1:C_E1 + QUAD], nlc, comb[:],
                                           ALU.mult, ALU.add).then_inc(comb_done, 1)
            dve.wait_ge(wb_ps, 1)
            nc.vector.tensor_copy(wbc[:], ps[:, 7, 64:64 + BATCH * ZONES]).then_inc(wbc_done, 1)
            dve.wait_ge(wbc_done, 1)

            def wb_zone(e, e2, par):
                dve.wait_ge(raw_in[par], 32 * (e2 + 1))
                dve.wait_ge(hs_free, H_BUFS + UZ * (e - 1) if not isinstance(e, int) or e else H_BUFS)
                for b in range(BATCH):
                    nc.vector.tensor_scalar(wbH[:, par, b, :], wb_raw[:, par, :], wsc(b, e), None,
                                            ALU.mult).then_inc(wbh_done, 1)
                dve.wait_ge(wbh_done, BATCH * (e + 1))
                for b in range(BATCH):
                    last = nc.vector.scalar_tensor_tensor(wbL[:, par, b, :], wb_raw[:, par, :], wsc(b, e),
                                                          wbH[:, par, b, :], ALU.mult, ALU.subtract)
                last.then_inc(wb_split, 1)

            def wsc(b, e):
                return wbc[:, bass.ds(b * ZONES + e, 1)]

            wb_zone(0, 0, 0)

            def split_turn(it, last):
                for s in range(2 * UZ):
                    n, buf = 2 * UZ * it + s, s % H_BUFS
                    dve.wait_ge(gelu_done, n + 1)
                    dve.wait_ge(hs_free, n + 1)
                    nc.vector.tensor_copy(hH[:, buf, :], h[:, s % 2, :]).then_inc(hh_done, 1)
                    dve.wait_ge(hh_done, n + 1)
                    nc.vector.tensor_tensor(hL[:, buf, :], h[:, s % 2, :], hH[:, buf, :],
                                            ALU.subtract).then_inc(split_done, 1)
                    if s == UZ // 2:
                        wb_zone(2 * it + 1, it, 1)
                    if s == UZ + UZ // 2 and not last:
                        wb_zone(2 * it + 2, it + 1, 0)

            with dve.Fori(0, ZONES // 2 - 1) as it:
                split_turn(it, False)
            split_turn(ZONES // 2 - 1, True)

            def reduce_unit(v, k, par):
                tt, j = k // GJ, k % GJ
                half, col = tt // FC, j * FC + tt % FC
                for sh in range(2):
                    dve.wait_ge(max_done, 2 * v + sh + 1)
                    nc.vector.tensor_reduce(part_max[:, half, col, sh:sh + 1], ps[:, B_MAX + sh, :], AX.X,
                                            ALU.max).then_inc(red_done, 1)
                if k % 16 == 15:
                    dve.wait_ge(red_done, 2 * v + 2)
                    nc.vector.tensor_reduce(neg_max[:, half, :], part_max[:, half, :, :], AX.X, ALU.max,
                                            negate=True).then_inc(neg_done, 1)

            def max_split(hx, half):
                dve.wait_ge(negt_done, hx + 1)
                nc.vector.tensor_copy(maxH[:, half, :], ps[0:16, B_MISC, 0:P]).then_inc(maxh_done, 1)
                dve.wait_ge(maxh_done, hx + 1)
                nc.vector.tensor_tensor(maxL[:, half, :], ps[0:16, B_MISC, 0:P], maxH[:, half, :],
                                        ALU.subtract).then_inc(maxl_done, 1)

            for v in range(LEAD):
                reduce_unit(v, v % UG, 0)
                if v == 19:
                    max_split(0, 0)
                if v in BACK:
                    c = BACK.index(v)
                    r = slice(c * FC, (c + 1) * FC)
                    dve.wait_ge(zt_done, c + 1)
                    nc.vector.tensor_tensor(RES[:, r, :].rearrange("p n d -> p (n d)"), ps[:, B_PV, :],
                                            X[:, r, :].rearrange("p n d -> p (n d)"), ALU.add).then_inc(res_done, 1)

            def turn(it, last):
                for s in range(PAIR):
                    for u in range(2):
                        o = LEAD + 2 * s + u
                        if last and 2 * PAIR * it + o >= ALL_UNITS:
                            continue
                        reduce_unit(2 * PAIR * it + o, o % UG, (o // UG) % 2)
                    done = LEAD + 2 * s - 2
                    if done % 16 == 0 and not (last and 2 * PAIR * it + done > ALL_UNITS):
                        hx = done // 16 - 1
                        max_split(4 * it + hx, hx % 2)
                    if s % TB == 2 and s >= TB:
                        reciprocals(4 * it + s // TB - 1, (s // TB - 1) % 2)
                reciprocals(4 * it + 3, 1)

            def reciprocals(a, th):
                dve.wait_ge(a_out, a + 1)
                dve.wait_ge(u_free, a + 1)
                dve.sem_inc(dve_waited, 1)
                nc.vector.stream_shuffle(den[:, th, :], A[:, th, :], [DV + i % DV for i in range(QUAD)]).then_inc(den_done, 1)
                dve.wait_ge(den_done, a + 1)
                nc.vector.reciprocal(rden[:, th, :], den[:, th, :]).then_inc(rden_done, 1)

            with dve.Fori(0, PAIRS - 1) as it:
                turn(it, False)
            turn(PAIRS - 1, True)

            for c in range(CHUNKS):
                dve.wait_ge(std_done, c + 1)
                link(nc.vector.reciprocal(rms, sd))
                nc.vector.scalar_tensor_tensor(rms, ps[:, 2 + c % 2, :], limit[:, 0:1], rms, ALU.is_le,
                                               ALU.mult).then_inc(rms_done, 1)
                dve.wait_ge(rms_done, c + 1)
                dve.wait_ge(at_out, c + 1)
                if c >= 2:
                    dve.wait_ge(o_ps, c - 1)
                nc.vector.scalar_tensor_tensor(an[c % 2], at, 1.0 - LAMBDA_INIT, rms, ALU.mult,
                                               ALU.mult).then_inc(an_done, 1)
                dve.wait_ge(o_ps, c + 1)
                r = RES[:, c * FC:(c + 1) * FC, :].rearrange("p n d -> p (n d)")
                nc.vector.tensor_tensor(r, ps[:, 4 + c % 2, :], r, ALU.add).then_inc(o_done, 1)

        @block.tensor
        def _(pe):
            mm = nc.tensor.matmul
            pe.wait_ge(c_in, 16)
            for c in range(CHUNKS):
                pe.wait_ge(xn_done, FC * (c + 1))
                for k in range(FC):
                    last = nc.tensor.transpose(ps[:, c, k * P:(k + 1) * P], XN[:, c * FC + k, :], ident)
                last.then_inc(xt_done, 1)
            for b in range(BATCH):
                for k in range(TB):
                    last = mm(ps[:, 7, b:b + 1], XN[:, b * TB + k, :], ones[:, 0:1], start=(k == 0), stop=(k == TB - 1))
            last.then_inc(pool_ps, 1)

            def three(o, lh, ll, rh, rl, start, stop):
                mm(o, lh, rh, start=start, stop=False)
                mm(o, lh, rl, start=False, stop=False)
                return mm(o, ll, rh, start=False, stop=stop)

            pe.wait_ge(w_split, 1)

            def project(m):
                kind, c = (m // CB) % 2, (m // (2 * CB)) * CB + m % CB
                for r in range(2):
                    k = 2 * m + r
                    w = 2 * kind + r
                    pe.wait_ge(xl_done, c + 1)
                    if k >= 3:
                        pe.wait_ge(rot_done, k - 2)
                    t = slice(c * BANK, (c + 1) * BANK)
                    three(ps[:, 4 + k % 3, :], wH[:, w, :], wL[:, w, :], xnH[:, t], xnL[:, t],
                          True, True).then_inc(proj_done, 1)

            for m in range(2):
                project(m)
            pe.wait_ge(pool_sb, 1)
            pe.wait_ge(s_in, 16 * 6)
            mm(ps[0:ROUTER, 7, 8:8 + BATCH], w1_in[:], pooled[:], start=True, stop=True).then_inc(hid_ps, 1)
            pe.wait_ge(lam_prod, 1)
            pe.wait_ge(hid_sb, 1)
            mm(ps[:, 7, 32:34], cst[0:DQ, C_ONE:C_ONE + P], lam_p[:], start=True, stop=True).then_inc(lam_ps, 1)
            for m in range(2, 4):
                project(m)
            pe.wait_ge(lam_exp, 1)
            mm(ps[0:BATCH, 7, 16:16 + ZONES], hid[:], w2_in[:], start=True, stop=False)
            mm(ps[0:BATCH, 7, 16:16 + ZONES], cst[0:1, C_ONE:C_ONE + BATCH], b2_in[:], start=False,
               stop=True).then_inc(logit_ps, 1)
            for m in range(4, 8):
                project(m)
            for c in range(CHUNKS):
                for k in range(FC):
                    t = slice((c * FC + k) * P, (c * FC + k + 1) * P)
                    last = three(ps[:, c, k * P:(k + 1) * P], xnH[:, t], xnL[:, t], wH[:, 4, :], wL[:, 4, :], True, True)
                last.then_inc(v_done, 1)
            pe.wait_ge(wsel, 1)
            for b in range(BATCH):
                last = mm(ps[:, 7, 64 + b * ZONES:64 + (b + 1) * ZONES], cst[0:BATCH, C_SEL + b * P:C_SEL + (b + 1) * P],
                          rt[:, 48:56], start=True, stop=True)
            last.then_inc(wb_ps, 1)

            pe.wait_ge(v_out, CHUNKS)
            pe.wait_ge(id_done, 1)
            for c in range(CHUNKS):
                t = slice(c * BANK, (c + 1) * BANK)
                mm(ps[:, c, :], identR[:], xnH[:, t], start=True, stop=False, skip_group_check=True)
                last = mm(ps[:, c, :], identR[:], xnL[:, t], start=False, stop=False, skip_group_check=True)
            last.then_inc(hs_free, H_BUFS)

            def first(s, par):
                c, hh = (s % UZ) // 2, s % 2
                t = slice(c * BANK, (c + 1) * BANK)
                for k in range(2):
                    f = slice((2 * hh + k) * P, (2 * hh + k + 1) * P)
                    last = three(ps[:, 4 + 2 * (s % 2) + k, :], waH[:, par, f], waL[:, par, f], xnH[:, t], xnL[:, t],
                                 True, True)
                last.then_inc(g1_done, 1)

            def second(s, par, end):
                c, hh, buf = (s % UZ) // 2, s % 2, s % H_BUFS
                for k in range(2):
                    f = slice((2 * hh + k) * P, (2 * hh + k + 1) * P)
                    t = slice(k * BANK, (k + 1) * BANK)
                    for i, (l, r) in enumerate(((wbH, hH), (wbH, hL), (wbL, hH))):
                        last = mm(ps[:, c, :], l[:, par, c // CB, f], r[:, buf, t], start=False,
                                  stop=end and k == 1 and i == 2, skip_group_check=True)
                last.then_inc(hs_free, 1)

            pe.wait_ge(rot_done, 16)
            pe.wait_ge(wbc_done, 1)
            pe.wait_ge(wa_split, 1)
            first(0, 0)
            first(1, 0)

            def ffn_turn(it, last):
                for s in range(2 * UZ):
                    n = 2 * UZ * it + s
                    if s % UZ == 0:
                        pe.wait_ge(wb_split, 2 * it + s // UZ + 1)
                    pe.wait_ge(split_done, n + 1)
                    second(s, s // UZ, last and s >= UZ and s % 2 == 1)
                    if last and s + 2 >= 2 * UZ:
                        continue
                    if (s + 2) % UZ == 0:
                        pe.wait_ge(wa_split, 2 * it + (s + 2) // UZ + 1)
                    pe.wait_ge(gelu_done, n + 1)
                    first((s + 2) % (2 * UZ), ((s + 2) // UZ) % 2)

            with pe.Fori(0, ZONES // 2 - 1) as it:
                ffn_turn(it, False)
            ffn_turn(ZONES // 2 - 1, True)

            def scores_max(v, k, par, wait=True):
                tt, j = k // GJ, k % GJ
                for sh in range(2):
                    if wait:
                        pe.wait_ge(red_done, 2 * v - 1 + sh)
                    mm(ps[:, B_MAX + sh, :], Q[:, par, tt * P:(tt + 1) * P], K[:, par, j, sh * BANK:(sh + 1) * BANK],
                       start=True, stop=True).then_inc(max_done, 1)

            def max_transpose(hx, half, wait=True):
                pe.wait_ge(neg_done, hx + 1)
                if wait:
                    pe.wait_ge(maxl_done, hx)
                nc.tensor.transpose(ps[0:16, B_MISC, 0:P], neg_max[:, half, :], ident).then_inc(negt_done, 1)

            def scores(s, par, jj):
                th, st = s // TB, s % TB
                for j in (2 * jj, 2 * jj + 1):
                    last = mm(ps[:, j, :], K[:, par, j, st * P:(st + 1) * P], Q[:, par, th * BANK:(th + 1) * BANK],
                              start=True, stop=True)
                last.then_inc(st_done, 1)

            def probs_v(s, par):
                st = s % TB
                for j in range(GJ):
                    last = mm(ps[QUAD * j:QUAD * (j + 1), B_PV, :], Vg[:, par, st, j // 2, :], E[:, s % 2, j, :],
                              start=(st == 0), stop=(st == TB - 1), skip_group_check=True)
                last.then_inc(e_free, 1)

            pe.wait_ge(kq_in, 2 * 16 * (GJ + 1))
            pe.wait_ge(gelu_done, UNITS)
            for v in range(LEAD):
                scores_max(v, v, 0, v > 0)
                if v == 18:
                    max_transpose(0, 0, False)
                if v in BACK:
                    c = BACK.index(v)
                    pe.wait_ge(z_out, CHUNKS)
                    if c:
                        pe.wait_ge(res_done, c)
                    for k in range(FC):
                        last = nc.tensor.transpose(ps[:, B_PV, k * P:(k + 1) * P],
                                                   zT[:, (c * FC + k) * P:(c * FC + k + 1) * P], ident)
                    last.then_inc(zt_done, 1)
            pe.wait_ge(qmax_in, 32)
            scores(0, 0, 0)
            scores(0, 0, 1)
            pe.wait_ge(res_done, CHUNKS)
            pe.sem_inc(e_free, 2)

            def turn(it, last):
                for s in range(PAIR):
                    n, p = PAIR * it + s, s // STEPS
                    nxt = s + 1
                    ahead = not (last and nxt == PAIR)
                    for jj in range(2):
                        if ahead:
                            if jj == 0 and nxt % TB == 0:
                                pe.wait_ge(qmax_in, 32 * (4 * it + nxt // TB + 1))
                            pe.wait_ge(exp_done, 2 * n + jj + 1)
                            scores(nxt % STEPS, (nxt // STEPS) % 2, jj)
                        o = LEAD + 2 * s + jj
                        if not (last and 2 * PAIR * it + o >= ALL_UNITS):
                            if o % UG == 0:
                                pe.wait_ge(kq_in, 16 * (GJ + 1) * (2 * it + o // UG + 1))
                            scores_max(2 * PAIR * it + o, o % UG, (o // UG) % 2)
                    done = LEAD + 2 * s - 2
                    if done % 16 == 0 and not (last and 2 * PAIR * it + done > ALL_UNITS):
                        hx = done // 16 - 1
                        max_transpose(4 * it + hx, hx % 2)
                    if s % STEPS == 0:
                        pe.wait_ge(vg_done, 2 * it + p + 1)
                    if s % TB == 0 and s > 0:
                        pe.wait_ge(a_out, 4 * it + s // TB)
                    pe.wait_ge(exp_done, 2 * n + 2)
                    probs_v(s % STEPS, p)

            with pe.Fori(0, PAIRS - 1) as it:
                turn(it, False)
            turn(PAIRS - 1, True)

            pe.wait_ge(comb_done, 1)
            pe.wait_ge(u_free, 2 + 2 * GROUPS)
            pe.wait_ge(exp_done, 2 * ALL_STEPS)
            pe.wait_ge(red_done, 2 * ALL_UNITS)

            def heads_sum(c):
                b, th = c // CB, c % CB
                if c >= 2:
                    pe.wait_ge(sq_done, c - 1)
                for g in range(GB):
                    a = 2 * (b * GB + g) + th
                    last = mm(ps[QUAD * g:QUAD * (g + 1), c % 2, :], comb[:], U[:, a * BANK:(a + 1) * BANK],
                              start=True, stop=True)
                last.then_inc(at_ps, 1)

            heads_sum(0)
            for c in range(CHUNKS):
                if c + 1 < CHUNKS:
                    heads_sum(c + 1)
                pe.wait_ge(sq_done, c + 1)
                if c >= 2:
                    pe.wait_ge(rms_done, c - 1)
                mm(ps[:, 2 + c % 2, :], blocksum, sq, start=True, stop=True).then_inc(ms_ps, 1)
                pe.wait_ge(an_done, c + 1)
                if c >= 2:
                    pe.wait_ge(o_done, c - 1)
                for k in range(FC):
                    last = mm(ps[:, 4 + c % 2, k * P:(k + 1) * P], an[c % 2][:, k * P:(k + 1) * P], wo_in[:],
                              start=True, stop=True)
                last.then_inc(o_ps, 1)


def shape_constants():
    c = np.zeros((P, C_END), np.float32)
    r = np.arange(P)
    c[:, C_ID:C_ID + P] = np.eye(P)
    c[:, C_BLK:C_BLK + P] = (r[:, None] // DV == r[None, :] // DV)
    for j in range(GJ):
        for i in range(DV):
            c[QUAD * j + i, (C_E0 if j % 2 == 0 else C_E1) + (j // 2) * DV + i] = 1
    for b in range(BATCH):
        c[b, C_SEL + b * P:C_SEL + (b + 1) * P] = 1
    c[0:BATCH, C_TRI:C_TRI + 64] = (np.arange(ZONES)[None, :] < np.arange(ZONES)[:, None]).reshape(-1)
    c[:, C_ONE:] = 1
    inv_freq = np.float32(1) / np.float32(10000) ** (np.arange(0, DQ, 2, dtype=np.float32) / np.float32(DQ))
    pos = np.arange(SEQ, dtype=np.float32)
    freqs = np.repeat(pos[:, None] * inv_freq[None, :], 2, axis=-1).astype(np.float64)
    sv = (np.arange(0, DQ, 2, dtype=np.float32) + np.float32(0.4 * DQ)) / np.float32(1.4 * DQ)
    scale = sv[None, :].astype(np.float64) ** ((pos - SEQ // 2) / 512.0)[:, None]
    scale = np.concatenate([scale, scale], axis=-1)
    sign = np.where(np.arange(DQ) % 2 == 0, -1.0, 1.0)[None, :]
    q = scale * DQ ** -0.5
    t = np.stack([np.cos(freqs) * q, np.sin(freqs) * sign * q, np.cos(freqs) / scale, np.sin(freqs) * sign / scale])
    t = np.tile(t.transpose(2, 0, 1), (SUBHEADS, 1, 1)).astype(np.float32)
    return c, np.ascontiguousarray(t)


def kernel(**inputs):
    import concourse.bacc as bacc
    from concourse.bass_utils import run_bass_kernel_spmd

    g = {k: np.asarray(v) for k, v in inputs.items()}
    consts, tables = shape_constants()
    swap = np.arange(P) ^ 1
    wq, wk, wv = g["L0_attn_Wq"], g["L0_attn_Wk"], g["L0_attn_Wv"]
    arrays = {
        "x": g["L0_attn_x"].reshape(TOKENS, P),
        "wqkv": np.stack([wq.T, wq[swap].T, wk.T, wk[swap].T, wv.T], axis=1),
        "wo": g["L0_attn_Wo"].T,
        "lam": np.stack([g[f"L0_attn_lambda_{n}"] for n in ("q1", "k1", "q2", "k2")], axis=1),
        "w1": g["L0_ffn_W1"],
        "b1": g["L0_ffn_b1"].reshape(ROUTER, 1),
        "w2": g["L0_ffn_W2"],
        "b2": g["L0_ffn_b2"].reshape(1, ZONES),
        "wa": g["L0_ffn_Wa"],
        "wb": g["L0_ffn_Wb"].reshape(ZONES, FC, P, P).transpose(0, 2, 1, 3).reshape(ZONES, P, FF),
        "consts": consts,
        "tables": tables,
    }
    arrays = {f"in_{k}": np.ascontiguousarray(v) for k, v in arrays.items()}
    nc = bacc.Bacc("TRN2", target_bir_lowering=False, num_devices=1)
    args = [nc.dram_tensor(k, v.shape, mybir.dt.from_np(v.dtype), kind="ExternalInput").ap() for k, v in arrays.items()]
    out = nc.dram_tensor("out", (TOKENS, P), F32, kind="ExternalOutput").ap()
    build(nc, *args, out)
    r = run_bass_kernel_spmd(nc, [arrays], core_ids=[0])
    return r.results[0]["out"].reshape(BATCH, SEQ, P)
```

```python
from contextlib import ExitStack
import math

import numpy as np

import concourse.bass as bass
from concourse import mybir

ALU = mybir.AluOpType
ACT = mybir.ActivationFunctionType
F32 = mybir.dt.float32
F32R = mybir.dt.float32r
AX = mybir.AxisListType

P = 128
BATCH, SEQ = 2, 1024
TOKENS = BATCH * SEQ
TILES = TOKENS // P
TB = SEQ // P
BANK = 512
CHUNKS = TOKENS // BANK
CB = SEQ // BANK
HEADS, SUBHEADS, DQ, DV = 8, 16, 8, 16
LAMBDA_INIT = 0.8 - 0.6 * math.exp(-0.3)
EPS = 1e-5
LAMBDA_RANGE = 2.0 ** 46
SQRT_LEAST = 2.0 ** -110
FLT_MAX = float(np.finfo(np.float32).max)
QUAD = 32
GJ = P // QUAD
GB = SUBHEADS // GJ
GROUPS = BATCH * GB
PROD_ROWS = 3 * DQ
MAX_ROW = PROD_ROWS
ZONES, TOP_K, FF, ROUTER = 8, 3, 512, 32
FC = FF // P
UZ = CHUNKS * FC
UNITS = ZONES * UZ
H_LEAD = 3
H_BUFS = 4
ROT_BUFS = 6
STEPS = SEQ // BANK * TB
ALL_STEPS = GROUPS * STEPS
UG = TB * GJ
ALL_UNITS = GROUPS * UG
BEHIND = 4
LEAD = 24
LEAD_AT = (0, 3, 6)
HALF_SLOTS = 2 * UG // 2 + 1
PAIR_SLOTS = 4 * HALF_SLOTS
SLOTS = 2 * ALL_UNITS + 2 * GROUPS
PAIR = 2 * STEPS
PAIRS = GROUPS // 2

ARENA = 206 * 1024

C_ID, C_E0, C_E1, C_SEL, C_TRI, C_ONE, C_END = 0, 128, 160, 192, 448, 512, 640

LEAD_RING, RING, B_PV = (4, 5), (4, 5, 7), 6
assert PAIR_SLOTS % len(RING) == 0


def unit_slot(v):
    return 2 * v + max(0, (v - 2) // (UG // 2))


LEAD_SLOTS = unit_slot(LEAD)
HEADS_AT = (20, 21, 29)
HEADS_BANK = RING + (0,)
AT_BANK = (1, 2, 3, 6)



def ring_bank(x):
    return LEAD_RING[x % 2] if x < LEAD_SLOTS else RING[x % 3]


def back_bank(c):
    return c if c < CHUNKS - 1 else B_PV


def lead_unit(u):
    return len(LEAD_AT) * (u // 8) + LEAD_AT.index(u % 8) if u >= 0 and u % 8 in LEAD_AT else None


def sum_chunk(u, after):
    c, rest = divmod(u - UZ - (FC - 1) - after, FC)
    return c if rest == 0 and 0 <= c < CHUNKS else None


def half_slot(hx):
    return HALF_SLOTS * hx + UG + 4




def build(nc, x, wqkv, wo, lam, w1, b1, w2, b2, wa, wb, consts, tables, out):
    with ExitStack() as ctx:
        def sem(name):
            return ctx.enter_context(nc.semaphore(name))

        ps = ctx.enter_context(nc.psum_tensor("ps", [P, 8, BANK], F32))

        base = (nc.sbuf_base + 31) // 32 * 32
        ctx.enter_context(nc.sbuf_tensor("arena", [P, ARENA // 4], F32))

        def region(start, *parts):
            at, made = start, []
            for name, shape, dt in parts:
                made.append(nc.alloc_sbuf_tensor_at(name, shape, dt, offset=base + at))
                at += (4 * math.prod(shape[1:]) + 31) // 32 * 32
            return made, at

        (X, cst, wo_in, identR, XN, V1, xnH, xnL, Q, lam_in, w1_in, b1_in, w2_in, b2_in, eps, stats, mv, rstd,
         ss, sd, sums, pooled, hid, rt, wbc, lam_p, lam_e, lt, epsc, limit, lnt, comb, part_max, neg_max, maxH, maxL, maxones), r1 = region(
            0,
            ("X", [P, TILES, P], F32), ("cst", [P, C_END], F32), ("wo_in", [P, P], F32),
            ("identR", [P, P], F32R), ("XN", [P, TILES, P], F32),
            ("V", [P, GROUPS * TB * 2 * QUAD], F32),
            ("xnH", [P, TOKENS], F32R), ("xnL", [P, TOKENS], F32R),
            ("Q", [P, 2, SEQ], F32R),
            ("lam_in", [DQ, 4], F32), ("w1_in", [P, ROUTER], F32), ("b1_in", [ROUTER, 1], F32),
            ("w2_in", [ROUTER, ZONES], F32), ("b2_in", [1, ZONES], F32), ("eps", [P, 1], F32),
            ("stats", [P, TILES, 6], F32), ("mv", [P, TILES, 2], F32), ("rstd", [P, TILES], F32),
            ("ss", [P, CHUNKS, QUAD], F32), ("sd", [P, CHUNKS, QUAD], F32), ("sums", [P, CHUNKS], F32), ("pooled", [P, BATCH], F32), ("hid", [ROUTER, BATCH], F32), ("rt", [BATCH, 256], F32),
            ("wbc", [P, BATCH * ZONES], F32), ("lam_p", [DQ, 2], F32), ("lam_e", [P, 2], F32),
            ("lt", [P, 8], F32), ("epsc", [P, 1], F32), ("limit", [P, 1], F32), ("lnt", [P, 2, TB], F32), ("comb", [P, QUAD], F32),
            ("part_max", [P, 2, 16, 2], F32), ("neg_max", [P, 2, 16], F32),
            ("maxH", [16, 2, P], F32R), ("maxL", [16, 2, P], F32R),
            ("maxones", [2, SEQ], F32R))
        (tab, rope), r2a = region(
            r1,
            ("tab", [P, 4, SEQ], F32),
            ("rope", [P, 2, BANK], F32))
        (K,), r2 = region(r1, ("K", [P, 2, GJ, SEQ], F32R))
        (ropeH, ropeL, w_in, wH, wL), r3 = region(
            r2, ("ropeH", [P, 2, SEQ], F32R), ("ropeL", [P, 2, SEQ], F32R),
            ("w_in", [P, 5, P], F32), ("wH", [P, 5, P], F32R), ("wL", [P, 5, P], F32R))
        (zT, Vg), r3b = region(
            r2, ("zT", [P, TOKENS], F32), ("Vg", [P, 2, TB, 2, QUAD], F32))
        (wa_raw, wb_raw, waH, waL, wbH, wbL, h, hH, hL, rot), r4 = region(
            r3, ("wa_raw", [P, 2, FF], F32), ("wb_raw", [P, 2, FF], F32),
            ("waH", [P, 2, FF], F32R), ("waL", [P, 2, FF], F32R),
            ("wbH", [P, 2, BATCH, FF], F32R), ("wbL", [P, 2, BATCH, FF], F32R),
            ("h", [P, 2, BANK], F32),
            ("hH", [P, H_BUFS, BANK], F32R), ("hL", [P, H_BUFS, BANK], F32R),
            ("rot", [P, ROT_BUFS, 2, BANK], F32))
        (E, A, AT, rsum, rb, rden, U), r4b = region(
            r3, ("E", [P, 2, GJ, BANK], F32), ("A", [P, 2, BANK], F32), ("AT", [P, 2, BANK], F32),
            ("rsum", [P, 2, BANK // QUAD], F32), ("rb", [P, 2, BANK], F32), ("rden", [P, 2, BANK], F32), ("U", [P, 2 * GROUPS * BANK], F32))
        assert r2a <= r2 and r3b <= r3 and max(r4, r4b) <= ARENA, (ARENA, r1, r2, r3, r4, r4b)
        V = V1[:].rearrange("p (g t h d) -> p g t h d", g=GROUPS, t=TB, h=2)
        ident = cst[:, C_ID:C_ID + P]
        ones = cst[:, C_ONE:C_ONE + P]
        RES = XN
        sq = [V1[:, k * BANK:(k + 1) * BANK] for k in range(2)]

        k_scr = nc.dram_tensor("k_scr", (GROUPS, GJ, PROD_ROWS, SEQ), F32, kind="Internal").ap()
        q_scr = nc.dram_tensor("q_scr", (GROUPS, P, SEQ), F32, kind="Internal").ap()

        x_in = [sem(f"x_in{b}") for b in range(BATCH)]
        c_in, w_arr, s_in, tab_in = sem("c_in"), sem("w_arr"), sem("s_in"), sem("tab_in")
        raw_in = [sem(f"raw_in{i}") for i in range(2)]
        scr_out, zero_out, ones_in, kq_in, qmax_in, out_done = (
            sem("scr_out"), sem("zero_out"), sem("ones_in"), sem("kq_in"), sem("qmax_in"), sem("out_done"))
        sp_waited, pool_waited = sem("sp_waited"), sem("pool_waited")
        fills, fills2 = sem("fills"), sem("fills2")
        warm, mv_done, sd_done, xn_done = sem("warm"), sem("mv_done"), sem("sd_done"), sem("xn_done")
        xt_done, xh_done, xl_done, id_done = sem("xt_done"), sem("xh_done"), sem("xl_done"), sem("id_done")
        wh_done, w_split = sem("wh_done"), sem("w_split")
        proj_done, rot_done, rope_done, ropeh_done, ropel_done = (
            sem("proj_done"), sem("rot_done"), sem("rope_done"), sem("ropeh_done"), sem("ropel_done"))
        v_done, v_out = sem("v_done"), sem("v_out")
        sums_done, pool_done, hid_ps, hid_sb, logit_ps, negl, expl, wsel, wb_ps, wbc_done = (
            sem("sums_done"), sem("pool_done"), sem("hid_ps"), sem("hid_sb"), sem("logit_ps"),
            sem("negl"), sem("expl"), sem("wsel"), sem("wb_ps"), sem("wbc_done"))
        lam_prod, lam_ps, lam_exp, comb_done = sem("lam_prod"), sem("lam_ps"), sem("lam_exp"), sem("comb_done")
        dch = sem("dch")
        wah_done, wa_split, wbh_done, wb_split = sem("wah_done"), sem("wa_split"), sem("wbh_done"), sem("wb_split")
        g1_done, gelu_done, hh_done, split_done, hs_free, z_out, zt_done, res_done = (
            sem("g1_done"), sem("gelu_done"), sem("hh_done"), sem("split_done"), sem("hs_free"),
            sem("z_out"), sem("zt_done"), sem("res_done"))
        slot_made, slot_read, neg_done, maxh_done = (
            sem("slot_made"), sem("slot_read"), sem("neg_done"), sem("maxh_done"))
        st_done, exp_done, e_free, vg_done, a_out, at_done, rsum_done, rb_done, rden_done, u_free = (
            sem("st_done"), sem("exp_done"), sem("e_free"), sem("vg_done"), sem("a_out"),
            sem("at_done"), sem("rsum_done"), sem("rb_done"), sem("rden_done"), sem("u_free"))
        heads_ps, sq_done, ss_done, std_done, rcp_done, rms_done, an_done, ant_ps, ant_done, o_ps, o_done = (
            sem("heads_ps"), sem("sq_done"), sem("ss_done"), sem("std_done"), sem("rcp_done"), sem("rms_done"),
            sem("an_done"), sem("ant_ps"), sem("ant_done"), sem("o_ps"), sem("o_done"))

        block = ctx.enter_context(nc.Block())

        @block.sync
        def _(sp):
            for b in range(BATCH):
                sp.dma_start(X[:, b * TB:(b + 1) * TB, :],
                             x[b * SEQ:(b + 1) * SEQ, :].rearrange("(n p) d -> p n d", p=P)).then_inc(x_in[b], 16)
            sp.dma_start(w_in[:], wqkv).then_inc(w_arr, 16)

            def raw_load(e, par):
                sp.sem_inc(sp_waited, 1)
                sp.dma_start(wa_raw[:, par, :], wa[e]).then_inc(raw_in[par], 16)
                sp.dma_start(wb_raw[:, par, :], wb[e]).then_inc(raw_in[par], 16)

            def raw_next(it, par):
                sp.wait_ge(wa_split, 2 * it + par + 1)
                sp.sem_inc(sp_waited, 1)
                sp.wait_ge(wb_split, BATCH * (2 * it + par + 1))
                raw_load(2 * it + par + 2, par)

            raw_load(0, 0)
            for dst, src in ((w1_in, w1), (b1_in, b1), (w2_in, w2), (b2_in, b2), (lam_in, lam), (wo_in, wo)):
                sp.dma_start(dst[:], src).then_inc(s_in, 16)
            raw_load(1, 1)
            sp.wait_ge(fills2, 1)
            for half in range(2):
                sp.dma_start(q_scr[half * GB:(half + 1) * GB].rearrange("g (j s r) t -> (g j) s r t", j=GJ, r=DQ)[:, 3],
                             ropeL[:, 1, :].bitcast(F32)).then_inc(zero_out, 16)
            for n in range(2 * BATCH):
                b, kind = n // 2, n % 2
                sp.wait_ge(ropel_done, CB * (n + 1))
                for part, places in ((ropeH, ((0, 1), (0, 2))[kind]), (ropeL, ((2,), (1,))[kind])):
                    for s in places:
                        if kind:
                            dst = k_scr[b * GB:(b + 1) * GB].rearrange("g j (s r) t -> (g j) s r t", r=DQ)[:, s]
                        else:
                            dst = q_scr[b * GB:(b + 1) * GB].rearrange("g (j s r) t -> (g j) s r t", j=GJ, r=DQ)[:, s]
                        sp.dma_start(dst, part[:, n % 2, :].bitcast(F32)).then_inc(scr_out, 16)
                sp.wait_ge(scr_out, 48 * (n + 1))
                if n == 2:
                    raw_next(0, 0)
            sp.wait_ge(zero_out, 32)
            sp.wait_ge(fills, 3)
            for par in range(2):
                for j in range(GJ):
                    r = QUAD * j + MAX_ROW
                    sp.dma_start(K[r:r + 2, par, j, :].bitcast(F32), maxones[0:2, :].bitcast(F32)).then_inc(ones_in, 16)

            def kq_load(i, par):
                sp.sem_inc(sp_waited, 1)
                for j in range(GJ):
                    sp.dma_start(K[QUAD * j:QUAD * j + PROD_ROWS, par, j, :].bitcast(F32), k_scr[i, j]).then_inc(kq_in, 16)
                sp.dma_start(Q[:, par, :].bitcast(F32), q_scr[i]).then_inc(kq_in, 16)

            raw_next(0, 1)
            sp.wait_ge(ones_in, 16 * 2 * GJ)
            kq_load(0, 0)
            sp.wait_ge(kq_in, 16 * (GJ + 1))
            kq_load(1, 1)
            with sp.Fori(1, ZONES // 2 - 1) as it:
                for par in range(2):
                    raw_next(it, par)
            sp.wait_ge(kq_in, 2 * 16 * (GJ + 1))

            def max_rows(i, slot, par, half):
                sp.wait_ge(slot_read, slot + 1)
                for part, row in ((maxH, MAX_ROW), (maxL, MAX_ROW + 1)):
                    dst = Q[row:P:QUAD, par, half * BANK:(half + 1) * BANK].bitcast(F32)
                    sp.dma_start(dst.rearrange("j (t c) -> j t c", c=P), part[:, half, :].bitcast(F32)).then_inc(qmax_in, 16)
                sp.wait_ge(qmax_in, 32 * (2 * i + half + 1))
                sp.sem_inc(sp_waited, 1)

            max_rows(0, half_slot(0), 0, 0)

            def turn(it, last):
                for p in range(2):
                    i = 2 * it + p
                    slot = [PAIR_SLOTS * it + half_slot(2 * p + k) for k in (1, 2)]
                    max_rows(i, SLOTS - 1 if last and p else slot[0], p, 1)
                    if not (last and p):
                        max_rows(i + 1, slot[1], 1 - p, 0)
                    if not last:
                        sp.wait_ge(st_done, 2 * STEPS * (i + 1))
                        kq_load(i + 2, p)
                        sp.wait_ge(kq_in, 16 * (GJ + 1) * (i + 3))
                        sp.sem_inc(sp_waited, 1)

            with sp.Fori(0, PAIRS - 1) as it:
                turn(it, False)
            turn(PAIRS - 1, True)
            for c in range(CHUNKS):
                sp.wait_ge(o_done, c + 1)
                sp.dma_start(out[c * BANK:(c + 1) * BANK, :].rearrange("(n p) d -> p n d", p=P),
                             RES[:, c * FC:(c + 1) * FC, :]).then_inc(out_done, 16)
            sp.wait_ge(out_done, 16 * CHUNKS)

        @block.gpsimd
        def _(pool):
            nc.gpsimd.memset(eps[:], EPS).then_inc(fills, 1)
            nc.gpsimd.memset(ropeL[:, 1, :].bitcast(F32), 0.0).then_inc(fills2, 1)
            nc.gpsimd.memset(V1[:], 1.0).then_inc(fills2, 1)
            pool.wait_ge(wh_done, 1)
            nc.gpsimd.tensor_tensor(wL[:], w_in[:], wH[:], ALU.subtract).then_inc(w_split, 1)

            def wa_zone(e, par, first):
                pool.wait_ge(raw_in[par], 32 * (e // 2 + 1) if first else 32 * (e + 1))
                if not first:
                    pool.wait_ge(g1_done, UZ * (2 * e + par - 1))
                    pool.sem_inc(pool_waited, 1)
                nc.gpsimd.tensor_copy(waH[:, par, :], wa_raw[:, par, :]).then_inc(wah_done, 1)
                pool.wait_ge(wah_done, e + 1 if first else 2 * e + par + 1)
                nc.gpsimd.tensor_tensor(waL[:, par, :], wa_raw[:, par, :], waH[:, par, :],
                                        ALU.subtract).then_inc(wa_split, 1)

            wa_zone(0, 0, True)
            wa_zone(1, 1, True)
            for m in range(2 * BATCH * CB):
                n, c = m // CB, m % CB
                pool.wait_ge(rot_done, 2 * (m + 1))
                if m >= 2:
                    pool.wait_ge(ropel_done, m - 1)
                nc.gpsimd.tensor_tensor(rope[:, m % 2, :], rot[:, m % ROT_BUFS, 0, :], rot[:, m % ROT_BUFS, 1, :],
                                        ALU.add).then_inc(rope_done, 1)
                pool.wait_ge(rope_done, m + 1)
                if n == 1 and c == 0:
                    pool.wait_ge(zero_out, 32)
                if n >= 2:
                    pool.wait_ge(scr_out, 48 * (n - 1))
                nc.gpsimd.tensor_copy(ropeH[:, n % 2, c * BANK:(c + 1) * BANK],
                                      rope[:, m % 2, :]).then_inc(ropeh_done, 1)
                pool.wait_ge(ropeh_done, m + 1)
                nc.gpsimd.tensor_tensor(ropeL[:, n % 2, c * BANK:(c + 1) * BANK], rope[:, m % 2, :],
                                        ropeH[:, n % 2, c * BANK:(c + 1) * BANK],
                                        ALU.subtract).then_inc(ropel_done, 1)
            pool.wait_ge(ropel_done, 2 * BATCH * CB)
            nc.gpsimd.memset(K[:].bitcast(F32), 0.0).then_inc(fills, 1)
            nc.gpsimd.memset(maxones[:].bitcast(F32), 1.0).then_inc(fills, 1)
            with pool.Fori(1, ZONES // 2) as e2:
                for par in range(2):
                    wa_zone(e2, par, False)

            pool.wait_ge(scr_out, 48 * 2 * BATCH)
            def v_group(i, par):
                pool.sem_inc(pool_waited, 1)
                nc.gpsimd.tensor_copy(Vg[:, par].rearrange("p a h d -> p (a h d)"),
                                      V1[:, bass.ts(i, TB * 2 * QUAD)]).then_inc(vg_done, 1)

            pool.wait_ge(v_out, CHUNKS)
            v_group(0, 0)
            v_group(1, 1)

            def turn(it, last):
                for p in range(2):
                    i = 2 * it + p
                    for th in range(2):
                        a = 2 * i + th
                        if last and a == 2 * GROUPS - 1:
                            continue
                        pool.wait_ge(rsum_done, a + 1)
                        pool.sem_inc(pool_waited, 1)
                        nc.gpsimd.tensor_copy(
                            rb[:, th, :].rearrange("p (k c) -> p k c", c=QUAD),
                            rsum[:, th, :].unsqueeze(2).broadcast_to([P, BANK // QUAD, QUAD])).then_inc(rb_done, 1)
                        pool.wait_ge(rden_done, a + 1)
                        nc.gpsimd.tensor_tensor(U[:, bass.ts(a, BANK)], A[:, th, :], rden[:, th, :],
                                                ALU.mult).then_inc(u_free, 1)
                    if not last:
                        pool.wait_ge(e_free, 2 + STEPS * (i + 1))
                        v_group(i + 2, p)

            pool.sem_inc(u_free, 2)
            with pool.Fori(0, PAIRS - 1) as it:
                turn(it, False)
            turn(PAIRS - 1, True)

        @block.scalar
        def _(act):
            act.dma_start(cst[:], consts).then_inc(c_in, 16)
            act.dma_start(tab[:], tables).then_inc(tab_in, 16)
            act.wait_ge(fills, 1)
            nc.scalar.activation(lt[:, 7:8], eps[:], ACT.Sqrt).then_inc(warm, 1)
            for b in range(BATCH):
                act.wait_ge(mv_done, TB * (b + 1))
                nc.scalar.activation(rstd[:, b * TB:(b + 1) * TB], mv[:, b * TB:(b + 1) * TB, 1], ACT.Sqrt,
                                     bias=eps[:, 0:1]).then_inc(sd_done, 1)
            act.wait_ge(w_arr, 16)
            nc.scalar.activation(wH[:], w_in[:], ACT.Copy).then_inc(wh_done, 1)
            act.wait_ge(c_in, 16)
            nc.scalar.activation(identR[:], ident, ACT.Copy).then_inc(id_done, 1)
            for c in range(CHUNKS):
                act.wait_ge(xt_done, c + 1)
                nc.scalar.activation(xnH[:, c * BANK:(c + 1) * BANK], ps[:, c, :], ACT.Copy).then_inc(xh_done, 1)
            def values_out(c):
                act.wait_ge(v_done, c + 1)
                for k in range(FC):
                    last = nc.scalar.activation(
                        V[:, c // CB * GB:(c // CB + 1) * GB, (c % CB) * FC + k, :, 0:DV],
                        ps[:, c, k * P:(k + 1) * P].rearrange("p (g h d) -> p g h d", g=GB, h=2), ACT.Copy)
                last.then_inc(v_out, 1)

            act.wait_ge(hid_ps, 1)
            act.wait_ge(s_in, 16 * 6)
            nc.scalar.activation(hid[:], ps[0:ROUTER, 7, 8:8 + BATCH], ACT.Tanh, bias=b1_in[:, 0:1]).then_inc(hid_sb, 1)
            act.wait_ge(lam_ps, 1)
            nc.scalar.activation(lam_e[:], ps[:, 7, 32:34], ACT.Exp).then_inc(lam_exp, 1)
            act.wait_ge(fills2, 2)
            for c in range(CB):
                values_out(c)
            act.wait_ge(negl, 1)
            nc.scalar.activation(rt[:, 8:16], ps[0:BATCH, 7, 16:16 + ZONES], ACT.Exp, bias=rt[:, 0:1]).then_inc(expl, 1)
            for c in range(CB, CHUNKS):
                values_out(c)

            def gelu(n, s):
                act.wait_ge(g1_done, n + 1)
                nc.scalar.activation(h[:, s % 2, :], ps[:, 6 + s % 2, :], ACT.Gelu_apprx_tanh).then_inc(gelu_done, 1)
                act.wait_ge(gelu_done, n + 1)
                act.wait_ge(hs_free, n + 1)
                nc.scalar.activation(hH[:, s % H_BUFS, :], h[:, s % 2, :], ACT.Copy).then_inc(hh_done, 1)

            def sums_copy(c):
                act.wait_ge(hs_free, H_BUFS + UNITS - UZ + FC * (c + 1))
                nc.scalar.activation(zT[:, c * BANK:(c + 1) * BANK], ps[:, c, :], ACT.Copy).then_inc(z_out, 1)

            gelu(0, 0)
            gelu(1, 1)

            def gelu_turn(it, last):
                for s in range(2 * UZ):
                    if not (last and s + 2 >= 2 * UZ):
                        act.wait_ge(split_done, 2 * UZ * it + s + 1)
                        gelu(2 * UZ * it + s + 2, s + 2)
                    if last and sum_chunk(s, 2) is not None:
                        sums_copy(sum_chunk(s, 2))

            with act.Fori(0, ZONES // 2 - 2) as it:
                gelu_turn(it, False)
            gelu_turn(ZONES // 2 - 2, False)
            act.wait_ge(scr_out, 48 * 2 * BATCH)
            gelu_turn(ZONES // 2 - 1, True)
            sums_copy(CHUNKS - 1)
            nc.scalar.activation(lt[:, 6:7], eps[:], ACT.Exp).then_inc(warm, 1)

            def exps(n, par):
                for jj in range(2):
                    act.wait_ge(st_done, 2 * n + jj + 1)
                    act.wait_ge(e_free, n + 1)
                    nc.scalar.activation(
                        E[:, par, 2 * jj:2 * jj + 2, :].rearrange("p j t -> p (j t)"),
                        ps[:, 2 * jj:2 * jj + 2, :].rearrange("p j t -> p (j t)"), ACT.Exp).then_inc(exp_done, 1)

            def turn(it, last):
                for s in range(1, PAIR + 1):
                    if not (last and s == PAIR):
                        exps(PAIR * it + s, s % 2)
                    if last and s - 1 in HEADS_AT:
                        squares(HEADS_AT.index(s - 1))
                    if last and s == PAIR:
                        roots(0, CHUNKS - 1)
                    if s % TB == 0:
                        evacuate(PAIR // TB * it + s // TB - 1, (s // TB - 1) % 2)

            def squares(c):
                act.wait_ge(heads_ps, c + 1)
                if c >= 2:
                    act.wait_ge(ss_done, c - 1)
                nc.scalar.activation(sq[c % 2], ps[:, HEADS_BANK[c], :], ACT.Square).then_inc(sq_done, 1)

            def roots(c, end):
                act.wait_ge(ss_done, end)
                nc.scalar.activation(sd[:, c:end, :], ss[:, c:end, :], ACT.Sqrt, scale=1.0 / DV,
                                     bias=epsc[:, 0:1]).then_inc(std_done, 1)

            def evacuate(a, th):
                act.wait_ge(e_free, 2 + TB * (a + 1))
                act.wait_ge(u_free, a + 1)
                nc.scalar.activation(A[:, th, :], ps[:, B_PV, :], ACT.Copy).then_inc(a_out, 1)

            exps(0, 0)
            with act.Fori(0, PAIRS - 1) as it:
                turn(it, False)
            turn(PAIRS - 1, True)

            def transposed_out(c):
                act.wait_ge(ant_ps, c + 1)
                nc.scalar.activation(zT[:, c * BANK:(c + 1) * BANK], ps[:, AT_BANK[c], :], ACT.Copy).then_inc(ant_done, 1)

            for c in range(CHUNKS - 1):
                transposed_out(c)
            squares(CHUNKS - 1)
            roots(CHUNKS - 1, CHUNKS)
            transposed_out(CHUNKS - 1)

        @block.vector
        def _(dve):
            chain = [0]

            def link(ins):
                chain[0] += 1
                ins.then_inc(dch, 1)
                dve.wait_ge(dch, chain[0])

            for b in range(BATCH):
                dve.wait_ge(x_in[b], 16)
                for n in range(b * TB, (b + 1) * TB):
                    last = nc.vector.bn_stats(stats[:, n, :], X[:, n, :])
                link(last)
                for n in range(b * TB, (b + 1) * TB):
                    nc.vector.bn_aggr(mv[:, n, :], stats[:, n, :]).then_inc(mv_done, 1)
            for b in range(BATCH):
                r, v, t = rstd[:, b * TB:(b + 1) * TB], lnt[:, 0, :], lnt[:, 1, :]
                dve.wait_ge(sd_done, b + 1)
                link(nc.vector.reciprocal(r, r))
                link(nc.vector.tensor_scalar(v, mv[:, b * TB:(b + 1) * TB, 1], EPS, -0.5, ALU.add, ALU.mult))
                link(nc.vector.tensor_tensor(t, r, r, ALU.mult))
                link(nc.vector.tensor_tensor(t, t, v, ALU.mult))
                link(nc.vector.scalar_tensor_tensor(r, t, 1.5, r, ALU.add, ALU.mult))
                for n in range(b * TB, (b + 1) * TB):
                    nc.vector.tensor_scalar(XN[:, n, :], X[:, n, :], mv[:, n, 0:1], rstd[:, n:n + 1],
                                            ALU.subtract, ALU.mult).then_inc(xn_done, 1)
            dve.wait_ge(s_in, 16 * 6)
            nc.vector.tensor_tensor(lam_p[:], lam_in[:, 0:4:2], lam_in[:, 1:4:2], ALU.mult).then_inc(lam_prod, 1)
            for c in range(CHUNKS):
                dve.wait_ge(xh_done, c + 1)
                nc.vector.tensor_tensor(xnL[:, c * BANK:(c + 1) * BANK], ps[:, c, :],
                                        xnH[:, c * BANK:(c + 1) * BANK], ALU.subtract).then_inc(xl_done, 1)
            for c in range(CHUNKS):
                nc.vector.tensor_reduce(sums[:, c:c + 1], ps[:, c, :], AX.X, ALU.add).then_inc(sums_done, 1)
            dve.wait_ge(sums_done, CHUNKS)
            link(nc.vector.tensor_tensor(pooled[:], sums[:, 0:CHUNKS:CB], sums[:, 1:CHUNKS:CB], ALU.add))
            nc.vector.tensor_scalar(pooled[:], pooled[:], 1.0 / SEQ, None, ALU.mult).then_inc(pool_done, 1)

            dve.wait_ge(tab_in, 16)

            def rotary(m):
                kind, c = (m // CB) % 2, m % CB
                for r in range(2):
                    k = 2 * m + r
                    dve.wait_ge(proj_done, k + 1)
                    if m >= ROT_BUFS:
                        dve.wait_ge(rope_done, m - ROT_BUFS + 1)
                    nc.vector.tensor_tensor(rot[:, m % ROT_BUFS, r, :], ps[:, 4 + k % 3, :],
                                            tab[:, 2 * kind + r, c * BANK:(c + 1) * BANK],
                                            ALU.mult).then_inc(rot_done, 1)

            for m in range(4):
                rotary(m)

            def wb_zone(e, e2, par, b, first=False):
                if b == 0:
                    dve.wait_ge(raw_in[par], 32 * (e2 + 1))
                    if not first:
                        dve.wait_ge(hs_free, H_BUFS + UZ * (e - 1))
                w = wbc[:, bass.ds(b * ZONES + e, 1)]
                nc.vector.tensor_scalar(wbH[:, par, b, :], wb_raw[:, par, :], w, None, ALU.mult).then_inc(wbh_done, 1)
                dve.wait_ge(wbh_done, BATCH * e + b + 1)
                nc.vector.scalar_tensor_tensor(wbL[:, par, b, :], wb_raw[:, par, :], w, wbH[:, par, b, :],
                                               ALU.mult, ALU.subtract).then_inc(wb_split, 1)

            dve.wait_ge(logit_ps, 1)
            nc.vector.tensor_reduce(rt[:, 0:1], ps[0:BATCH, 7, 16:16 + ZONES], AX.X, ALU.max,
                                    negate=True).then_inc(negl, 1)
            for m in range(4, 6):
                rotary(m)
            dve.wait_ge(expl, 1)
            e_, p_ = rt[:, 8:16], rt[:, 16:24]
            gt = rt[:, 64:128].rearrange("b (e j) -> b e j", j=ZONES)
            eq = rt[:, 128:192].rearrange("b (e j) -> b e j", j=ZONES)
            tri = cst[0:BATCH, C_TRI:C_TRI + 64].rearrange("b (e j) -> b e j", j=ZONES)
            pj = rt[:, 16:24].unsqueeze(1).broadcast_to([BATCH, ZONES, ZONES])
            pe_ = rt[:, 16:24].unsqueeze(2).broadcast_to([BATCH, ZONES, ZONES])
            link(nc.vector.tensor_reduce(rt[:, 1:2], e_, AX.X, ALU.add))
            link(nc.vector.reciprocal(rt[:, 2:3], rt[:, 1:2]))
            link(nc.vector.tensor_scalar(p_, e_, rt[:, 2:3], None, ALU.mult))
            link(nc.vector.tensor_tensor(gt, pj, pe_, ALU.is_gt))
            link(nc.vector.tensor_tensor(eq, pj, pe_, ALU.is_equal))
            link(nc.vector.tensor_tensor(eq, eq, tri, ALU.mult))
            link(nc.vector.tensor_tensor(gt, gt, eq, ALU.add))
            link(nc.vector.tensor_reduce(rt[:, 24:32], gt, AX.X, ALU.add))
            link(nc.vector.tensor_scalar(rt[:, 32:40], rt[:, 24:32], TOP_K - 0.5, None, ALU.is_lt))
            link(nc.vector.tensor_tensor(rt[:, 40:48], rt[:, 32:40], p_, ALU.mult))
            link(nc.vector.tensor_reduce(rt[:, 3:4], rt[:, 40:48], AX.X, ALU.add))
            link(nc.vector.reciprocal(rt[:, 4:5], rt[:, 3:4]))
            nc.vector.tensor_scalar(rt[:, 48:56], rt[:, 40:48], rt[:, 4:5], None, ALU.mult).then_inc(wsel, 1)
            rotary(6)
            dve.wait_ge(wb_ps, 1)
            nc.vector.tensor_copy(wbc[:], ps[:, 7, 64:64 + BATCH * ZONES]).then_inc(wbc_done, 1)
            dve.wait_ge(wbc_done, 1)
            for b in range(BATCH):
                wb_zone(0, 0, 0, b, True)
            rotary(7)
            dve.wait_ge(lam_exp, 1)
            nl, ab, cc, c2, nlc = (lt[:, k:k + 1] for k in range(5))
            link(nc.vector.scalar_tensor_tensor(nl, lam_e[:, 1:2], LAMBDA_INIT, lam_e[:, 0:1],
                                                ALU.subtract, ALU.subtract))
            link(nc.vector.tensor_scalar(ab, nl, -1.0, None, ALU.mult))
            link(nc.vector.tensor_tensor(ab, ab, nl, ALU.max))
            link(nc.vector.tensor_scalar(ab, ab, 1.0, None, ALU.add))
            link(nc.vector.reciprocal(cc, ab))
            link(nc.vector.tensor_scalar(cc, cc, LAMBDA_RANGE, 1.0, ALU.mult, ALU.min))
            link(nc.vector.tensor_tensor(c2, cc, cc, ALU.mult))
            link(nc.vector.tensor_scalar(epsc[:], c2, EPS, SQRT_LEAST, ALU.mult, ALU.max))
            link(nc.vector.tensor_scalar(limit[:], c2, FLT_MAX, None, ALU.mult))
            link(nc.vector.tensor_tensor(nlc, nl, cc, ALU.mult))
            link(nc.vector.tensor_scalar(comb[:], cst[:, C_E0:C_E0 + QUAD], cc, None, ALU.mult))
            nc.vector.scalar_tensor_tensor(comb[:], cst[:, C_E1:C_E1 + QUAD], nlc, comb[:],
                                           ALU.mult, ALU.add).then_inc(comb_done, 1)

            def reduce_bank(slot, x, half, col, sh):
                dve.wait_ge(slot_made, slot + 1)
                nc.vector.tensor_reduce(part_max[:, half, col, sh:sh + 1], ps[:, ring_bank(x), :], AX.X,
                                        ALU.max).then_inc(slot_read, 1)

            def max_split(hx, half, slot, x):
                dve.wait_ge(slot_made, slot + 1)
                nc.vector.tensor_copy(maxH[:, half, :], ps[0:16, ring_bank(x), 0:P]).then_inc(maxh_done, 1)
                dve.wait_ge(maxh_done, hx + 1)
                nc.vector.tensor_tensor(maxL[:, half, :], ps[0:16, ring_bank(x), 0:P], maxH[:, half, :],
                                        ALU.subtract).then_inc(slot_read, 1)

            def max_unit(it, o, last):
                if last and 2 * PAIR * it + o >= ALL_UNITS:
                    return
                x, k, h = unit_slot(o), o % UG, o // (UG // 2)
                base = PAIR_SLOTS * it
                for sh in range(2):
                    reduce_bank(base + x + sh, x + sh, h % 2, k % GJ * FC + k // GJ % FC, sh)
                if o % (UG // 2) == UG // 2 - 1:
                    dve.wait_ge(slot_read, base + x + 2)
                    nc.vector.tensor_reduce(neg_max[:, h % 2, :], part_max[:, h % 2, :, :], AX.X, ALU.max,
                                            negate=True).then_inc(neg_done, 1)
                if o % (UG // 2) == 1 and h:
                    max_split(4 * it + h - 1, (h - 1) % 2, base + half_slot(h - 1), half_slot(h - 1))
                if last and 2 * PAIR * it + o == ALL_UNITS - 1:
                    max_split(2 * GROUPS - 1, 1, SLOTS - 1, SLOTS - 1)

            def residual(c):
                r = slice(c * FC, (c + 1) * FC)
                dve.wait_ge(zt_done, c + 1)
                nc.vector.tensor_tensor(RES[:, r, :].rearrange("p n d -> p (n d)"), ps[:, back_bank(c), :],
                                        X[:, r, :].rearrange("p n d -> p (n d)"), ALU.add).then_inc(res_done, 1)

            def split_turn(it, lead, last):
                for s in range(2 * UZ):
                    n = 2 * UZ * it + s
                    dve.wait_ge(hh_done, n + 1)
                    nc.vector.tensor_tensor(hL[:, s % H_BUFS, :], h[:, s % 2, :], hH[:, s % H_BUFS, :],
                                            ALU.subtract).then_inc(split_done, 1)
                    if s in (FC, 2 * FC):
                        wb_zone(2 * it + 1, it, 1, s // FC - 1)
                    if s in (UZ + FC, UZ + 2 * FC) and not last:
                        wb_zone(2 * it + 2, it + 1, 0, (s - UZ) // FC - 1)
                    if lead and lead_unit(2 * UZ * last + s - 2) is not None:
                        max_unit(0, lead_unit(2 * UZ * last + s - 2), False)
                    if last and sum_chunk(s, 6) is not None:
                        residual(sum_chunk(s, 6))

            with dve.Fori(0, ZONES // 2 - 2) as it:
                split_turn(it, False, False)
            split_turn(ZONES // 2 - 2, True, False)
            split_turn(ZONES // 2 - 1, True, True)
            for u in range(4 * UZ - 2, 4 * UZ):
                if lead_unit(u) is not None:
                    max_unit(0, lead_unit(u), False)
            for c in range(2, CHUNKS):
                residual(c)
            for v in range(LEAD, LEAD + 2 * BEHIND):
                max_unit(0, v, False)

            def sums_out(a, th):
                dve.wait_ge(a_out, a + 2)
                nc.vector.transpose(AT[:, th, :], A[:, th, :]).then_inc(at_done, 1)
                dve.wait_ge(at_done, a + 1)
                nc.vector.reciprocal(rsum[:, th, :],
                                     AT[:, th, :].rearrange("p (k c) -> p k c", c=QUAD)[:, :, DV]).then_inc(rsum_done, 1)

            def reciprocals(a, th):
                dve.wait_ge(rb_done, a + 1)
                nc.vector.transpose(rden[:, th, :], rb[:, th, :]).then_inc(rden_done, 1)

            def normalise_last():
                a = 2 * GROUPS - 1
                dve.wait_ge(rsum_done, a + 1)
                nc.vector.tensor_tensor(rb[:, 1, :].rearrange("p (k c) -> p k c", c=QUAD),
                                        AT[:, 1, :].rearrange("p (k c) -> p k c", c=QUAD),
                                        rsum[:, 1, :].unsqueeze(2).broadcast_to([P, BANK // QUAD, QUAD]),
                                        ALU.mult).then_inc(rb_done, 1)
                dve.wait_ge(rb_done, a + 1)
                nc.vector.transpose(U[:, a * BANK:(a + 1) * BANK], rb[:, 1, :]).then_inc(u_free, 1)

            def square_sums(c):
                dve.wait_ge(sq_done, c + 1)
                nc.vector.tensor_reduce(ss[:, c, :], sq[c % 2].rearrange("p (n v) -> p n v", v=DV), AX.X,
                                        ALU.add).then_inc(ss_done, 1)

            def shares(c, end):
                last_one = int(end == CHUNKS)
                dve.wait_ge(std_done, last_one + 1)
                nc.vector.reciprocal(sd[:, c:end, :], sd[:, c:end, :]).then_inc(rcp_done, 1)
                dve.wait_ge(rcp_done, last_one + 1)
                nc.vector.scalar_tensor_tensor(sd[:, c:end, :], ss[:, c:end, :], limit[:, 0:1], sd[:, c:end, :],
                                               ALU.is_le, ALU.mult).then_inc(rms_done, 1)
                dve.wait_ge(rms_done, last_one + 1)

            def normalise(c):
                nc.vector.scalar_tensor_tensor(
                    X[:, c * FC:(c + 1) * FC, :].rearrange("p n (h v) -> p (n h) v", v=DV),
                    ps[:, HEADS_BANK[c], :].rearrange("p (n v) -> p n v", v=DV), 1.0 - LAMBDA_INIT,
                    sd[:, c, :].unsqueeze(2).broadcast_to([P, QUAD, DV]), ALU.mult, ALU.mult).then_inc(an_done, 1)

            def add_product(c):
                dve.wait_ge(o_ps, c + 1)
                r = RES[:, c * FC:(c + 1) * FC, :].rearrange("p n d -> p (n d)")
                nc.vector.tensor_tensor(r, ps[:, HEADS_BANK[c], :], r, ALU.add).then_inc(o_done, 1)

            def turn(it, last):
                for s in range(PAIR):
                    for u in range(2):
                        max_unit(it, LEAD + 2 * BEHIND + 2 * s + u, last)
                    half = s // TB
                    if last and s == HEADS_AT[0] - BEHIND:
                        square_sums(0)
                        square_sums(1)
                    if last and s == PAIR - BEHIND:
                        square_sums(2)
                        shares(0, CHUNKS - 1)
                        normalise(0)
                    if s % TB == TB - BEHIND + 1:
                        sums_out(PAIR // TB * it + half, half % 2)
                    if s % TB == TB - 1 and not (last and s == PAIR - 1):
                        reciprocals(PAIR // TB * it + half, half % 2)

            with dve.Fori(0, PAIRS - 1) as it:
                turn(it, False)
            turn(PAIRS - 1, True)

            normalise_last()
            normalise(1)
            normalise(2)
            add_product(0)
            square_sums(3)
            add_product(1)
            shares(CHUNKS - 1, CHUNKS)
            normalise(3)
            add_product(2)
            add_product(3)

        @block.tensor
        def _(pe):
            mm = nc.tensor.matmul
            pe.wait_ge(c_in, 16)
            for c in range(CHUNKS):
                pe.wait_ge(xn_done, FC * (c + 1))
                for k in range(FC):
                    last = nc.tensor.transpose(ps[:, c, k * P:(k + 1) * P], XN[:, c * FC + k, :], ident)
                last.then_inc(xt_done, 1)
            def three(o, lh, ll, rh, rl, start, stop):
                mm(o, lh, rh, start=start, stop=False)
                mm(o, lh, rl, start=False, stop=False)
                return mm(o, ll, rh, start=False, stop=stop)

            pe.wait_ge(w_split, 1)

            def project(m):
                kind, c = (m // CB) % 2, (m // (2 * CB)) * CB + m % CB
                for r in range(2):
                    k = 2 * m + r
                    w = 2 * kind + r
                    pe.wait_ge(xl_done, c + 1)
                    if k >= 3:
                        pe.wait_ge(rot_done, k - 2)
                    t = slice(c * BANK, (c + 1) * BANK)
                    three(ps[:, 4 + k % 3, :], wH[:, w, :], wL[:, w, :], xnH[:, t], xnL[:, t],
                          True, True).then_inc(proj_done, 1)

            def values(c):
                for k in range(FC):
                    t = slice((c * FC + k) * P, (c * FC + k + 1) * P)
                    last = three(ps[:, c, k * P:(k + 1) * P], xnH[:, t], xnL[:, t], wH[:, 4, :], wL[:, 4, :], True, True)
                last.then_inc(v_done, 1)

            for m in range(2):
                project(m)
            pe.wait_ge(pool_done, 1)
            pe.wait_ge(s_in, 16 * 6)
            mm(ps[0:ROUTER, 7, 8:8 + BATCH], w1_in[:], pooled[:], start=True, stop=True).then_inc(hid_ps, 1)
            pe.wait_ge(lam_prod, 1)
            pe.wait_ge(hid_sb, 1)
            mm(ps[:, 7, 32:34], cst[0:DQ, C_ONE:C_ONE + P], lam_p[:], start=True, stop=True).then_inc(lam_ps, 1)
            for m in range(2, 4):
                values(m - 2)
                project(m)
            pe.wait_ge(lam_exp, 1)
            mm(ps[0:BATCH, 7, 16:16 + ZONES], hid[:], w2_in[:], start=True, stop=False)
            mm(ps[0:BATCH, 7, 16:16 + ZONES], cst[0:1, C_ONE:C_ONE + BATCH], b2_in[:], start=False,
               stop=True).then_inc(logit_ps, 1)
            for m in range(4, 6):
                values(m - 2)
                project(m)
            project(6)
            pe.wait_ge(wsel, 1)
            for b in range(BATCH):
                last = mm(ps[:, 7, 64 + b * ZONES:64 + (b + 1) * ZONES], cst[0:BATCH, C_SEL + b * P:C_SEL + (b + 1) * P],
                          rt[:, 48:56], start=True, stop=True)
            last.then_inc(wb_ps, 1)
            project(7)

            pe.wait_ge(v_out, CHUNKS)
            pe.wait_ge(id_done, 1)
            for c in range(CHUNKS):
                t = slice(c * BANK, (c + 1) * BANK)
                mm(ps[:, c, :], identR[:], xnH[:, t], start=True, stop=False, skip_group_check=True)
                last = mm(ps[:, c, :], identR[:], xnL[:, t], start=False, stop=False, skip_group_check=True)
            last.then_inc(hs_free, H_BUFS)

            def first(s, par):
                c, f = s % UZ // FC, s % FC
                t = slice(c * BANK, (c + 1) * BANK)
                f = slice(f * P, (f + 1) * P)
                three(ps[:, 6 + s % 2, :], waH[:, par, f], waL[:, par, f], xnH[:, t], xnL[:, t],
                      True, True).then_inc(g1_done, 1)

            def second(s, par, end):
                c, f, buf = s % UZ // FC, s % FC, s % H_BUFS
                fs = slice(f * P, (f + 1) * P)
                for i, (l, r) in enumerate(((wbH, hH), (wbH, hL), (wbL, hH))):
                    last = mm(ps[:, c, :], l[:, par, c // CB, fs], r[:, buf, :], start=False,
                              stop=end and f == FC - 1 and i == 2, skip_group_check=True)
                last.then_inc(hs_free, 1)

            pe.wait_ge(rot_done, 15)
            pe.wait_ge(wa_split, 1)
            first(0, 0)
            pe.wait_ge(wbc_done, 1)
            first(1, 0)
            pe.wait_ge(gelu_done, 1)
            first(2, 0)

            def ffn_turn(it, lead, last):
                for s in range(2 * UZ):
                    n, a = 2 * UZ * it + s, s + H_LEAD
                    if not (last and a >= 2 * UZ):
                        if a % UZ == 0:
                            pe.wait_ge(wa_split, 2 * it + a // UZ + 1)
                        pe.wait_ge(gelu_done, n + H_LEAD - 1)
                        first(a % (2 * UZ), a // UZ % 2)
                    if s % UZ == 0:
                        pe.wait_ge(wb_split, BATCH * (2 * it + s // UZ + 1))
                    pe.wait_ge(split_done, n + 1)
                    second(s, s // UZ, last and s >= UZ)
                    if lead and lead_unit(2 * UZ * last + s) is not None:
                        for sh in range(2):
                            max_slot(0, lead_unit(2 * UZ * last + s), sh, False)
                    if last and sum_chunk(s, 3) is not None:
                        back(sum_chunk(s, 3))

            def back(c):
                pe.wait_ge(z_out, c + 1)
                for k in range(FC):
                    last = nc.tensor.transpose(ps[:, back_bank(c), k * P:(k + 1) * P],
                                               zT[:, (c * FC + k) * P:(c * FC + k + 1) * P], ident)
                last.then_inc(zt_done, 1)

            def half_transpose(hx, half, slot, x):
                pe.wait_ge(neg_done, hx + 1)
                pe.wait_ge(slot_read, slot - (1 if x < LEAD_SLOTS else 2))
                nc.tensor.transpose(ps[0:16, ring_bank(x), 0:P], neg_max[:, half, :], ident).then_inc(slot_made, 1)

            def max_slot(it, o, sh, last):
                if last and 2 * PAIR * it + o >= ALL_UNITS:
                    return
                x, k, g, h = unit_slot(o), o % UG, o // UG, o // (UG // 2)
                base = PAIR_SLOTS * it
                if k == 0 and sh == 0:
                    pe.wait_ge(kq_in, 16 * (GJ + 1) * (2 * it + g + 1))
                back_to = 1 if x < LEAD_SLOTS else 2
                if x + sh > back_to:
                    pe.wait_ge(slot_read, base + x + sh - back_to)
                mm(ps[:, ring_bank(x + sh), :], Q[:, g % 2, k // GJ * P:(k // GJ + 1) * P],
                   K[:, g % 2, k % GJ, sh * BANK:(sh + 1) * BANK], start=True, stop=True).then_inc(slot_made, 1)
                if o % (UG // 2) == 1 and h and sh:
                    half_transpose(4 * it + h - 1, (h - 1) % 2, base + half_slot(h - 1), half_slot(h - 1))
                if last and 2 * PAIR * it + o == ALL_UNITS - 1 and sh:
                    half_transpose(2 * GROUPS - 1, 1, SLOTS - 1, SLOTS - 1)

            def heads_sum(c):
                b, th = c // CB, c % CB
                if c == 0:
                    pe.wait_ge(comb_done, 1)
                    pe.wait_ge(slot_read, SLOTS)
                pe.wait_ge(u_free, 2 + 2 * (b * GB + GB - 1) + th + 1)
                for k in range(FC):
                    for g in range(GB):
                        t = (2 * (b * GB + g) + th) * BANK + k * P
                        last = mm(ps[:, HEADS_BANK[c], k * P + g * QUAD:k * P + (g + 1) * QUAD], U[:, t:t + P], comb[:],
                                  start=True, stop=True)
                last.then_inc(heads_ps, 1)

            def scores(s, par, jj):
                th, st = s // TB, s % TB
                for j in (2 * jj, 2 * jj + 1):
                    last = mm(ps[:, j, :], K[:, par, j, st * P:(st + 1) * P], Q[:, par, th * BANK:(th + 1) * BANK],
                              start=True, stop=True)
                last.then_inc(st_done, 1)

            def probs_v(s, par):
                st = s % TB
                for j in range(GJ):
                    last = mm(ps[QUAD * j:QUAD * (j + 1), B_PV, :], Vg[:, par, st, j // 2, :], E[:, s % 2, j, :],
                              start=(st == 0), stop=(st == TB - 1), skip_group_check=True)
                last.then_inc(e_free, 1)

            with pe.Fori(0, ZONES // 2 - 2) as it:
                ffn_turn(it, False, False)
            ffn_turn(ZONES // 2 - 2, True, False)
            ffn_turn(ZONES // 2 - 1, True, True)
            pe.wait_ge(qmax_in, 32)
            pe.wait_ge(res_done, 2)
            scores(0, 0, 0)
            pe.wait_ge(z_out, CHUNKS)
            pe.wait_ge(res_done, CHUNKS - 1)
            scores(0, 0, 1)
            pe.wait_ge(gelu_done, UNITS)
            back(CHUNKS - 1)
            pe.wait_ge(res_done, CHUNKS)
            pe.wait_ge(slot_read, LEAD_SLOTS)
            pe.sem_inc(e_free, 2)
            pe.sem_inc(a_out, 1)

            def turn(it, last):
                for s in range(PAIR):
                    n, p = PAIR * it + s, s // STEPS
                    nxt = s + 1
                    ahead = not (last and nxt == PAIR)
                    o = LEAD + 2 * s
                    for jj in range(2):
                        max_slot(it, o, jj, last)
                        if ahead:
                            if jj == 0 and nxt % TB == 0:
                                pe.wait_ge(qmax_in, 32 * (4 * it + nxt // TB + 1))
                            pe.wait_ge(exp_done, 2 * n + jj + 1)
                            scores(nxt % STEPS, (nxt // STEPS) % 2, jj)
                    for sh in range(2):
                        max_slot(it, o + 1, sh, last)
                    if last and s in HEADS_AT:
                        heads_sum(HEADS_AT.index(s))
                    if s % STEPS == 0:
                        pe.wait_ge(vg_done, 2 * it + p + 1)
                    if s % TB == 0:
                        pe.wait_ge(a_out, PAIR // TB * it + s // TB + 1)
                    pe.wait_ge(exp_done, 2 * n + 2)
                    probs_v(s % STEPS, p)

            with pe.Fori(0, PAIRS - 1) as it:
                turn(it, False)
            turn(PAIRS - 1, True)

            def transpose_back(c):
                pe.wait_ge(an_done, c + 1)
                for k in range(FC):
                    last = nc.tensor.transpose(ps[:, AT_BANK[c], k * P:(k + 1) * P], X[:, c * FC + k, :], ident)
                last.then_inc(ant_ps, 1)

            def product(c):
                pe.wait_ge(ant_done, c + 1)
                for k in range(FC):
                    last = mm(ps[:, HEADS_BANK[c], k * P:(k + 1) * P], zT[:, (c * FC + k) * P:(c * FC + k + 1) * P],
                              wo_in[:], start=True, stop=True)
                last.then_inc(o_ps, 1)

            pe.wait_ge(exp_done, 2 * ALL_STEPS)
            transpose_back(0)
            transpose_back(1)
            product(0)
            transpose_back(2)
            product(1)
            heads_sum(3)
            product(2)
            pe.wait_ge(a_out, 2 * GROUPS + 1)
            transpose_back(3)
            product(3)


def shape_constants():
    c = np.zeros((P, C_END), np.float32)
    r = np.arange(P)
    c[:, C_ID:C_ID + P] = np.eye(P)
    for j in range(GJ):
        for i in range(DV):
            c[QUAD * j + i, (C_E0 if j % 2 == 0 else C_E1) + (j // 2) * DV + i] = 1
    for b in range(BATCH):
        c[b, C_SEL + b * P:C_SEL + (b + 1) * P] = 1
    c[0:BATCH, C_TRI:C_TRI + 64] = (np.arange(ZONES)[None, :] < np.arange(ZONES)[:, None]).reshape(-1)
    c[:, C_ONE:] = 1
    inv_freq = np.float32(1) / np.float32(10000) ** (np.arange(0, DQ, 2, dtype=np.float32) / np.float32(DQ))
    pos = np.arange(SEQ, dtype=np.float32)
    freqs = np.repeat(pos[:, None] * inv_freq[None, :], 2, axis=-1).astype(np.float64)
    sv = (np.arange(0, DQ, 2, dtype=np.float32) + np.float32(0.4 * DQ)) / np.float32(1.4 * DQ)
    scale = sv[None, :].astype(np.float64) ** ((pos - SEQ // 2) / 512.0)[:, None]
    scale = np.concatenate([scale, scale], axis=-1)
    sign = np.where(np.arange(DQ) % 2 == 0, -1.0, 1.0)[None, :]
    q = scale * DQ ** -0.5
    t = np.stack([np.cos(freqs) * q, np.sin(freqs) * sign * q, np.cos(freqs) / scale, np.sin(freqs) * sign / scale])
    t = np.tile(t.transpose(2, 0, 1), (SUBHEADS, 1, 1)).astype(np.float32)
    return c, np.ascontiguousarray(t)


def kernel(**inputs):
    import concourse.bacc as bacc
    from concourse.bass_utils import run_bass_kernel_spmd

    g = {k: np.asarray(v) for k, v in inputs.items()}
    consts, tables = shape_constants()
    swap = np.arange(P) ^ 1
    wq, wk, wv = g["L0_attn_Wq"], g["L0_attn_Wk"], g["L0_attn_Wv"]
    arrays = {
        "x": g["L0_attn_x"].reshape(TOKENS, P),
        "wqkv": np.stack([wq.T, wq[swap].T, wk.T, wk[swap].T, wv.T], axis=1),
        "wo": g["L0_attn_Wo"].T,
        "lam": np.stack([g[f"L0_attn_lambda_{n}"] for n in ("q1", "k1", "q2", "k2")], axis=1),
        "w1": g["L0_ffn_W1"],
        "b1": g["L0_ffn_b1"].reshape(ROUTER, 1),
        "w2": g["L0_ffn_W2"],
        "b2": g["L0_ffn_b2"].reshape(1, ZONES),
        "wa": g["L0_ffn_Wa"],
        "wb": g["L0_ffn_Wb"].reshape(ZONES, FC, P, P).transpose(0, 2, 1, 3).reshape(ZONES, P, FF),
        "consts": consts,
        "tables": tables,
    }
    arrays = {f"in_{k}": np.ascontiguousarray(v) for k, v in arrays.items()}
    nc = bacc.Bacc("TRN2", target_bir_lowering=False, num_devices=1)
    args = [nc.dram_tensor(k, v.shape, mybir.dt.from_np(v.dtype), kind="ExternalInput").ap() for k, v in arrays.items()]
    out = nc.dram_tensor("out", (TOKENS, P), F32, kind="ExternalOutput").ap()
    build(nc, *args, out)
    r = run_bass_kernel_spmd(nc, [arrays], core_ids=[0])
    return r.results[0]["out"].reshape(BATCH, SEQ, P)
```

```python
from contextlib import ExitStack
import math

import numpy as np

import concourse.bass as bass
from concourse import mybir

ALU = mybir.AluOpType
ACT = mybir.ActivationFunctionType
F32 = mybir.dt.float32
F32R = mybir.dt.float32r
AX = mybir.AxisListType

P = 128
BATCH, SEQ = 2, 1024
TOKENS = BATCH * SEQ
TILES = TOKENS // P
TB = SEQ // P
BANK = 512
CHUNKS = TOKENS // BANK
CB = SEQ // BANK
HEADS, SUBHEADS, DQ, DV = 8, 16, 8, 16
LAMBDA_INIT = 0.8 - 0.6 * math.exp(-0.3)
EPS = 1e-5
LAMBDA_RANGE = 2.0 ** 46
SQRT_LEAST = 2.0 ** -110
FLT_MAX = float(np.finfo(np.float32).max)
QUAD = 32
GJ = P // QUAD
GB = SUBHEADS // GJ
GROUPS = BATCH * GB
PROD_ROWS = 3 * DQ
MAX_ROW = PROD_ROWS
ZONES, TOP_K, FF, ROUTER = 8, 3, 512, 32
FC = FF // P
UZ = CHUNKS * FC
UNITS = ZONES * UZ
H_LEAD = 3
H_BUFS = 4
ROT_BUFS = 6
WARM_UP = 30
STEPS = SEQ // BANK * TB
ALL_STEPS = GROUPS * STEPS
UG = TB * GJ
ALL_UNITS = GROUPS * UG
BEHIND = 4
LEAD = 24
LEAD_AT = (0, 3, 6)
HALF_SLOTS = UG + 1
PAIR_SLOTS = 4 * HALF_SLOTS
SLOTS = 2 * ALL_UNITS + 2 * GROUPS
NB = BANK // QUAD
HALF_U = NB * DV
PAIR = 2 * STEPS
PAIRS = GROUPS // 2

ARENA = 206 * 1024

C_ID, C_E0, C_E1, C_SEL, C_TRI, C_ONE, C_END = 0, 128, 192, 256, 512, 576, 704

LEAD_RING, RING, B_PV = (4, 5), (4, 5, 7), 6
assert PAIR_SLOTS % len(RING) == 0


def unit_slot(v):
    return 2 * v + max(0, (v - 2) // (UG // 2))


LEAD_SLOTS = unit_slot(LEAD)
HEADS_AT = (21, 22, 29)
TAIL_ORDER = (0, 1, 3, 2)
HEADS_BANK = RING + (0,)
O_BANK = (1, 2, 3, B_PV)


def ring_bank(x):
    return LEAD_RING[x % 2] if x < LEAD_SLOTS else RING[x % 3]


def proj_bank(k):
    return 4 + (k % 3 if k < 14 else k % 2)


def back_bank(c):
    return c if c < CHUNKS - 1 else B_PV


def lead_unit(u):
    return len(LEAD_AT) * (u // 8) + LEAD_AT.index(u % 8) if u >= 0 and u % 8 in LEAD_AT else None


def sum_chunk(u, after):
    c, rest = divmod(u - UZ - (FC - 1) - after, FC)
    return c if rest == 0 and 0 <= c < CHUNKS else None


def half_slot(hx):
    return HALF_SLOTS * hx + UG + 4


def build(nc, x, wqkv, wo, lam, w1, b1, w2, b2, wa, wb, consts, tables, out):
    with ExitStack() as ctx:
        def sem(name):
            return ctx.enter_context(nc.semaphore(name))

        ps = ctx.enter_context(nc.psum_tensor("ps", [P, 8, BANK], F32))

        base = (nc.sbuf_base + 31) // 32 * 32
        ctx.enter_context(nc.sbuf_tensor("arena", [P, ARENA // 4], F32))

        def region(start, *parts):
            at, made = start, []
            for name, shape, dt in parts:
                made.append(nc.alloc_sbuf_tensor_at(name, shape, dt, offset=base + at))
                at += (4 * math.prod(shape[1:]) + 31) // 32 * 32
            return made, at

        (X, cst, wo_in, identR, XN, V1, xnH, xnL, Q, lam_in, w1_in, b1_in, w2_in, b2_in, eps, stats, mv, rstd, shift,
         ss, sd, sums, pooled, hid, rt, wbc, lam_p, lam_e, lt, epsc, limit, lnt, comb,
         part_max, neg_max, maxH, maxL, maxones), r1 = region(
            0,
            ("X", [P, TILES, P], F32), ("cst", [P, C_END], F32), ("wo_in", [P, P], F32),
            ("identR", [P, P], F32R), ("XN", [P, TILES, P], F32),
            ("V", [P, GROUPS * TB * 2 * QUAD], F32),
            ("xnH", [P, TOKENS], F32R), ("xnL", [P, TOKENS], F32R),
            ("Q", [P, 2, SEQ], F32R),
            ("lam_in", [DQ, 4], F32), ("w1_in", [P, ROUTER], F32), ("b1_in", [ROUTER, 1], F32),
            ("w2_in", [ROUTER, ZONES], F32), ("b2_in", [1, ZONES], F32), ("eps", [P, 1], F32),
            ("stats", [P, TILES, 6], F32), ("mv", [P, TILES, 2], F32), ("rstd", [P, TILES], F32),
            ("shift", [P, TILES], F32),
            ("ss", [P, CHUNKS, QUAD], F32), ("sd", [P, CHUNKS, QUAD], F32), ("sums", [P, CHUNKS], F32),
            ("pooled", [P, BATCH], F32), ("hid", [ROUTER, BATCH], F32), ("rt", [BATCH, 256], F32),
            ("wbc", [P, BATCH * ZONES], F32), ("lam_p", [DQ, 2], F32), ("lam_e", [P, 2], F32),
            ("lt", [P, 8], F32), ("epsc", [P, 1], F32), ("limit", [P, 1], F32), ("lnt", [P, 2, TB], F32),
            ("comb", [P, 2 * QUAD], F32),
            ("part_max", [P, 2, 16, 2], F32), ("neg_max", [P, 2, 16], F32),
            ("maxH", [16, 2, P], F32R), ("maxL", [16, 2, P], F32R),
            ("maxones", [2, SEQ], F32R))
        (tab, rope), r2a = region(
            r1,
            ("tab", [P, 4, SEQ], F32),
            ("rope", [P, 2, BANK], F32))
        (K,), r2 = region(r1, ("K", [P, 2, GJ, SEQ], F32R))
        (ropeH, ropeL, w_in, wH, wL), r3 = region(
            r2, ("ropeH", [P, 2, SEQ], F32R), ("ropeL", [P, 2, SEQ], F32R),
            ("w_in", [P, 5, P], F32), ("wH", [P, 5, P], F32R), ("wL", [P, 5, P], F32R))
        (zT, Vg), r3b = region(
            r2, ("zT", [P, TOKENS], F32), ("Vg", [P, 2, TB, 2, QUAD], F32))
        (wa_raw, wb_raw, waH, waL, wbH, wbL, h, hH, hL, rot), r4 = region(
            r3, ("wa_raw", [P, 2, FF], F32), ("wb_raw", [P, 2, FF], F32),
            ("waH", [P, 2, FF], F32R), ("waL", [P, 2, FF], F32R),
            ("wbH", [P, 2, BATCH, FF], F32R), ("wbL", [P, 2, BATCH, FF], F32R),
            ("h", [P, 2, BANK], F32),
            ("hH", [P, H_BUFS, BANK], F32R), ("hL", [P, H_BUFS, BANK], F32R),
            ("rot", [P, ROT_BUFS, 2, BANK], F32))
        (E, A, AT, rsum, U), r4b = region(
            r3, ("E", [P, 2, GJ, BANK], F32), ("A", [P, 2, BANK], F32), ("AT", [P, 2, BANK], F32),
            ("rsum", [P, 2, NB], F32),
            ("U", [P, 2 * GROUPS * HALF_U], F32))
        assert r2a <= r2 and r3b <= r3 and max(r4, r4b) <= ARENA, (ARENA, r1, r2, r3, r4, r4b)
        V = V1[:].rearrange("p (g t h d) -> p g t h d", g=GROUPS, t=TB, h=2)
        ident = cst[:, C_ID:C_ID + P]
        ones = cst[:, C_ONE:C_ONE + P]
        RES = XN
        sq = [V1[:, k * BANK:(k + 1) * BANK] for k in range(2)]

        k_scr = nc.dram_tensor("k_scr", (GROUPS, GJ, PROD_ROWS, SEQ), F32, kind="Internal").ap()
        q_scr = nc.dram_tensor("q_scr", (GROUPS, P, SEQ), F32, kind="Internal").ap()

        def products(th):
            return AT[:, th, :].rearrange("p (k c) -> p k c", c=QUAD)[:, :, 0:DV]

        x_in = [sem(f"x_in{b}") for b in range(BATCH)]
        c_in, w_arr, s_in, tab_in = sem("c_in"), sem("w_arr"), sem("s_in"), sem("tab_in")
        raw_in = [sem(f"raw_in{i}") for i in range(2)]
        scr_out, zero_out, ones_in, kq_in, qmax_in, out_done = (
            sem("scr_out"), sem("zero_out"), sem("ones_in"), sem("kq_in"), sem("qmax_in"), sem("out_done"))
        sp_waited, pool_waited = sem("sp_waited"), sem("pool_waited")
        fills, fills2 = sem("fills"), sem("fills2")
        zeros_done, warm, mv_done, sd_done, shift_done, xn_done, xa_done = (
            sem("zeros_done"), sem("warm"), sem("mv_done"), sem("sd_done"), sem("shift_done"), sem("xn_done"), sem("xa_done"))
        xt_done, xh_done, xl_done, id_done = sem("xt_done"), sem("xh_done"), sem("xl_done"), sem("id_done")
        wh_done, w_split = sem("wh_done"), sem("w_split")
        proj_done, rot_done, rope_done, ropeh_done, ropel_done = (
            sem("proj_done"), sem("rot_done"), sem("rope_done"), sem("ropeh_done"), sem("ropel_done"))
        v_done, v_out = sem("v_done"), sem("v_out")
        sums_done, pool_done, hid_ps, hid_sb, logit_ps, negl, expl, wsel, wb_ps, wbc_done = (
            sem("sums_done"), sem("pool_done"), sem("hid_ps"), sem("hid_sb"), sem("logit_ps"),
            sem("negl"), sem("expl"), sem("wsel"), sem("wb_ps"), sem("wbc_done"))
        lam_prod, lam_ps, lam_exp, comb_done = sem("lam_prod"), sem("lam_ps"), sem("lam_exp"), sem("comb_done")
        dch = sem("dch")
        wah_done, wa_split, wbh_done, wb_split = sem("wah_done"), sem("wa_split"), sem("wbh_done"), sem("wb_split")
        g1_done, gelu_done, hh_done, split_done, hs_free, z_out, zt_done, res_done = (
            sem("g1_done"), sem("gelu_done"), sem("hh_done"), sem("split_done"), sem("hs_free"),
            sem("z_out"), sem("zt_done"), sem("res_done"))
        slot_made, slot_read, neg_done, maxh_done = (
            sem("slot_made"), sem("slot_read"), sem("neg_done"), sem("maxh_done"))
        st_done, exp_done, e_free, vg_done, a_out, at_done, rsum_done, u_free = (
            sem("st_done"), sem("exp_done"), sem("e_free"), sem("vg_done"), sem("a_out"),
            sem("at_done"), sem("rsum_done"), sem("u_free"))
        heads_ps, sq_done, ss_done, std_done, rcp_done, rms_done, an_done, ant_done, o_ps, o_done = (
            sem("heads_ps"), sem("sq_done"), sem("ss_done"), sem("std_done"), sem("rcp_done"), sem("rms_done"),
            sem("an_done"), sem("ant_done"), sem("o_ps"), sem("o_done"))

        block = ctx.enter_context(nc.Block())

        @block.sync
        def _(sp):
            for b in range(BATCH):
                sp.dma_start(X[:, b * TB:(b + 1) * TB, :],
                             x[b * SEQ:(b + 1) * SEQ, :].rearrange("(n p) d -> p n d", p=P)).then_inc(x_in[b], 16)

            def raw_load(e, par):
                sp.sem_inc(sp_waited, 1)
                sp.dma_start(wa_raw[:, par, :], wa[e]).then_inc(raw_in[par], 16)
                sp.dma_start(wb_raw[:, par, :], wb[e]).then_inc(raw_in[par], 16)

            def raw_next(it, par):
                sp.wait_ge(wa_split, 2 * it + par + 1)
                sp.sem_inc(sp_waited, 1)
                sp.wait_ge(wb_split, BATCH * (2 * it + par + 1))
                raw_load(2 * it + par + 2, par)

            raw_load(0, 0)
            for dst, src in ((w1_in, w1), (b1_in, b1), (w2_in, w2), (b2_in, b2), (lam_in, lam), (wo_in, wo)):
                sp.dma_start(dst[:], src).then_inc(s_in, 16)
            raw_load(1, 1)
            sp.wait_ge(fills2, 1)
            for half in range(2):
                sp.dma_start(q_scr[half * GB:(half + 1) * GB].rearrange("g (j s r) t -> (g j) s r t", j=GJ, r=DQ)[:, 3],
                             ropeL[:, 1, :].bitcast(F32)).then_inc(zero_out, 16)
            for n in range(2 * BATCH):
                b, kind = n // 2, n % 2
                sp.wait_ge(ropel_done, CB * (n + 1))
                for part, places in ((ropeH, ((0, 1), (0, 2))[kind]), (ropeL, ((2,), (1,))[kind])):
                    for s in places:
                        if kind:
                            dst = k_scr[b * GB:(b + 1) * GB].rearrange("g j (s r) t -> (g j) s r t", r=DQ)[:, s]
                        else:
                            dst = q_scr[b * GB:(b + 1) * GB].rearrange("g (j s r) t -> (g j) s r t", j=GJ, r=DQ)[:, s]
                        sp.dma_start(dst, part[:, n % 2, :].bitcast(F32)).then_inc(scr_out, 16)
                sp.wait_ge(scr_out, 48 * (n + 1))
                if n == 2:
                    raw_next(0, 0)
            sp.wait_ge(zero_out, 32)
            sp.wait_ge(fills, 3)
            for par in range(2):
                for j in range(GJ):
                    r = QUAD * j + MAX_ROW
                    sp.dma_start(K[r:r + 2, par, j, :].bitcast(F32), maxones[0:2, :].bitcast(F32)).then_inc(ones_in, 16)

            def kq_load(i, par):
                sp.sem_inc(sp_waited, 1)
                for j in range(GJ):
                    sp.dma_start(K[QUAD * j:QUAD * j + PROD_ROWS, par, j, :].bitcast(F32), k_scr[i, j]).then_inc(kq_in, 16)
                sp.dma_start(Q[:, par, :].bitcast(F32), q_scr[i]).then_inc(kq_in, 16)

            raw_next(0, 1)
            sp.wait_ge(ones_in, 16 * 2 * GJ)
            kq_load(0, 0)
            sp.wait_ge(kq_in, 16 * (GJ + 1))
            kq_load(1, 1)
            with sp.Fori(1, ZONES // 2 - 1) as it:
                for par in range(2):
                    raw_next(it, par)
            sp.wait_ge(kq_in, 2 * 16 * (GJ + 1))

            def max_rows(i, slot, par, half):
                sp.wait_ge(slot_read, slot + 1)
                for part, row in ((maxH, MAX_ROW), (maxL, MAX_ROW + 1)):
                    dst = Q[row:P:QUAD, par, half * BANK:(half + 1) * BANK].bitcast(F32)
                    sp.dma_start(dst.rearrange("j (t c) -> j t c", c=P), part[:, half, :].bitcast(F32)).then_inc(qmax_in, 16)
                sp.wait_ge(qmax_in, 32 * (2 * i + half + 1))
                sp.sem_inc(sp_waited, 1)

            max_rows(0, half_slot(0), 0, 0)

            def turn(it, last):
                for p in range(2):
                    i = 2 * it + p
                    slot = [PAIR_SLOTS * it + half_slot(2 * p + k) for k in (1, 2)]
                    max_rows(i, SLOTS - 1 if last and p else slot[0], p, 1)
                    if not (last and p):
                        max_rows(i + 1, slot[1], 1 - p, 0)
                    if not last:
                        sp.wait_ge(st_done, 2 * STEPS * (i + 1))
                        kq_load(i + 2, p)
                        sp.wait_ge(kq_in, 16 * (GJ + 1) * (i + 3))
                        sp.sem_inc(sp_waited, 1)

            with sp.Fori(0, PAIRS - 1) as it:
                turn(it, False)
            turn(PAIRS - 1, True)
            for k, c in enumerate(TAIL_ORDER):
                sp.wait_ge(o_done, k + 1)
                sp.dma_start(out[c * BANK:(c + 1) * BANK, :].rearrange("(n p) d -> p n d", p=P),
                             RES[:, c * FC:(c + 1) * FC, :]).then_inc(out_done, 16)
            sp.wait_ge(out_done, 16 * CHUNKS)

        @block.gpsimd
        def _(pool):
            nc.gpsimd.memset(eps[:], EPS).then_inc(fills, 1)
            nc.gpsimd.memset(ropeL[:, 1, :].bitcast(F32), 0.0).then_inc(fills2, 1)
            nc.gpsimd.memset(V1[:], 1.0).then_inc(fills2, 1)
            pool.wait_ge(wh_done, 1)
            nc.gpsimd.tensor_tensor(wL[:], w_in[:], wH[:], ALU.subtract).then_inc(w_split, 1)

            def wa_zone(e, par, first):
                pool.wait_ge(raw_in[par], 32 * (e // 2 + 1) if first else 32 * (e + 1))
                if not first:
                    pool.wait_ge(g1_done, UZ * (2 * e + par - 1))
                    pool.sem_inc(pool_waited, 1)
                nc.gpsimd.tensor_copy(waH[:, par, :], wa_raw[:, par, :]).then_inc(wah_done, 1)
                pool.wait_ge(wah_done, e + 1 if first else 2 * e + par + 1)
                nc.gpsimd.tensor_tensor(waL[:, par, :], wa_raw[:, par, :], waH[:, par, :],
                                        ALU.subtract).then_inc(wa_split, 1)

            wa_zone(0, 0, True)
            wa_zone(1, 1, True)
            for m in range(2 * BATCH * CB):
                n, c = m // CB, m % CB
                pool.wait_ge(rot_done, 2 * (m + 1))
                if m >= 2:
                    pool.wait_ge(ropel_done, m - 1)
                nc.gpsimd.tensor_tensor(rope[:, m % 2, :], rot[:, m % ROT_BUFS, 0, :], rot[:, m % ROT_BUFS, 1, :],
                                        ALU.add).then_inc(rope_done, 1)
                pool.wait_ge(rope_done, m + 1)
                if n == 1 and c == 0:
                    pool.wait_ge(zero_out, 32)
                if n >= 2:
                    pool.wait_ge(scr_out, 48 * (n - 1))
                nc.gpsimd.tensor_copy(ropeH[:, n % 2, c * BANK:(c + 1) * BANK],
                                      rope[:, m % 2, :]).then_inc(ropeh_done, 1)
                pool.wait_ge(ropeh_done, m + 1)
                nc.gpsimd.tensor_tensor(ropeL[:, n % 2, c * BANK:(c + 1) * BANK], rope[:, m % 2, :],
                                        ropeH[:, n % 2, c * BANK:(c + 1) * BANK],
                                        ALU.subtract).then_inc(ropel_done, 1)
            pool.wait_ge(ropel_done, 2 * BATCH * CB)
            nc.gpsimd.memset(K[:].bitcast(F32), 0.0).then_inc(fills, 1)
            nc.gpsimd.memset(maxones[:].bitcast(F32), 1.0).then_inc(fills, 1)
            with pool.Fori(1, ZONES // 2) as e2:
                for par in range(2):
                    wa_zone(e2, par, False)

            pool.wait_ge(scr_out, 48 * 2 * BATCH)
            def v_group(i, par):
                pool.sem_inc(pool_waited, 1)
                nc.gpsimd.tensor_copy(Vg[:, par].rearrange("p a h d -> p (a h d)"),
                                      V1[:, bass.ts(i, TB * 2 * QUAD)]).then_inc(vg_done, 1)

            pool.wait_ge(v_out, CHUNKS)
            v_group(0, 0)
            v_group(1, 1)

            def turn(it, last):
                for p in range(2):
                    i = 2 * it + p
                    for th in range(2):
                        a = 2 * i + th
                        if last and a == 2 * GROUPS - 1:
                            continue
                        pool.wait_ge(rsum_done, a + 1)
                        nc.gpsimd.tensor_tensor(
                            U[:, bass.ts(a, HALF_U)].rearrange("p (k c) -> p k c", c=DV), products(th),
                            rsum[:, th, :].unsqueeze(2).broadcast_to([P, NB, DV]), ALU.mult).then_inc(u_free, 1)
                    if not last:
                        pool.wait_ge(e_free, 2 + STEPS * (i + 1))
                        v_group(i + 2, p)

            pool.sem_inc(u_free, 2)
            with pool.Fori(0, PAIRS - 1) as it:
                turn(it, False)
            turn(PAIRS - 1, True)

        @block.scalar
        def _(act):
            act.dma_start(cst[:], consts).then_inc(c_in, 16)
            act.dma_start(w_in[:], wqkv).then_inc(w_arr, 16)
            act.dma_start(tab[:], tables).then_inc(tab_in, 16)
            act.wait_ge(fills, 1)
            nc.scalar.activation(lt[:, 7:8], eps[:], ACT.Sqrt).then_inc(warm, 1)
            for b in range(BATCH):
                act.wait_ge(mv_done, TB * (b + 1))
                nc.scalar.activation(rstd[:, b * TB:(b + 1) * TB], mv[:, b * TB:(b + 1) * TB, 1], ACT.Sqrt,
                                     bias=eps[:, 0:1]).then_inc(sd_done, 1)
            act.wait_ge(w_arr, 16)
            nc.scalar.activation(wH[:], w_in[:], ACT.Copy).then_inc(wh_done, 1)
            act.wait_ge(c_in, 16)
            for c in range(CHUNKS):
                if c < BATCH:
                    act.wait_ge(shift_done, c + 1)
                    for n in range(c * TB + FC, (c + 1) * TB):
                        nc.scalar.activation(XN[:, n, :], X[:, n, :], ACT.Identity, scale=rstd[:, n:n + 1],
                                             bias=shift[:, n:n + 1]).then_inc(xa_done, 1)
                act.wait_ge(xt_done, c + 1)
                nc.scalar.activation(xnH[:, c * BANK:(c + 1) * BANK], ps[:, c, :], ACT.Copy).then_inc(xh_done, 1)
            nc.scalar.activation(identR[:], ident, ACT.Copy).then_inc(id_done, 1)
            def values_out(c):
                act.wait_ge(v_done, c + 1)
                for k in range(FC):
                    last = nc.scalar.activation(
                        V[:, c // CB * GB:(c // CB + 1) * GB, (c % CB) * FC + k, :, 0:DV],
                        ps[:, c, k * P:(k + 1) * P].rearrange("p (g h d) -> p g h d", g=GB, h=2), ACT.Copy)
                last.then_inc(v_out, 1)

            act.wait_ge(fills2, 2)
            values_out(0)
            act.wait_ge(hid_ps, 1)
            act.wait_ge(s_in, 16 * 6)
            nc.scalar.activation(hid[:], ps[0:ROUTER, 7, 8:8 + BATCH], ACT.Tanh, bias=b1_in[:, 0:1]).then_inc(hid_sb, 1)
            act.wait_ge(lam_ps, 1)
            nc.scalar.activation(lam_e[:], ps[:, 7, 32:34], ACT.Exp).then_inc(lam_exp, 1)
            values_out(1)
            act.wait_ge(negl, 1)
            nc.scalar.activation(rt[:, 8:16], ps[0:BATCH, 7, 16:16 + ZONES], ACT.Exp, bias=rt[:, 0:1]).then_inc(expl, 1)
            for c in range(2, CHUNKS):
                values_out(c)

            def gelu(n, s):
                act.wait_ge(g1_done, n + 1)
                nc.scalar.activation(h[:, s % 2, :], ps[:, 6 + s % 2, :], ACT.Gelu_apprx_tanh).then_inc(gelu_done, 1)
                act.wait_ge(gelu_done, n + 1)
                act.wait_ge(hs_free, n + 1)
                nc.scalar.activation(hH[:, s % H_BUFS, :], h[:, s % 2, :], ACT.Copy).then_inc(hh_done, 1)

            def sums_copy(c):
                act.wait_ge(hs_free, H_BUFS + UNITS - UZ + FC * (c + 1))
                nc.scalar.activation(zT[:, c * BANK:(c + 1) * BANK], ps[:, c, :], ACT.Copy).then_inc(z_out, 1)

            gelu(0, 0)
            gelu(1, 1)

            def gelu_turn(it, last):
                for s in range(2 * UZ):
                    if not (last and s + 2 >= 2 * UZ):
                        act.wait_ge(split_done, 2 * UZ * it + s + 1)
                        gelu(2 * UZ * it + s + 2, s + 2)
                    if last and sum_chunk(s, 2) is not None:
                        sums_copy(sum_chunk(s, 2))

            with act.Fori(0, ZONES // 2 - 2) as it:
                gelu_turn(it, False)
            gelu_turn(ZONES // 2 - 2, False)
            act.wait_ge(scr_out, 48 * 2 * BATCH)
            gelu_turn(ZONES // 2 - 1, True)
            nc.scalar.activation(lt[:, 6:7], eps[:], ACT.Exp).then_inc(warm, 1)
            sums_copy(CHUNKS - 1)

            def exps(n, par):
                for jj in range(2):
                    act.wait_ge(st_done, 2 * n + jj + 1)
                    act.wait_ge(e_free, n + 1)
                    nc.scalar.activation(
                        E[:, par, 2 * jj:2 * jj + 2, :].rearrange("p j t -> p (j t)"),
                        ps[:, 2 * jj:2 * jj + 2, :].rearrange("p j t -> p (j t)"), ACT.Exp).then_inc(exp_done, 1)

            def turn(it, last):
                for s in range(1, PAIR + 1):
                    if not (last and s == PAIR):
                        exps(PAIR * it + s, s % 2)
                    if last and s - 1 in HEADS_AT:
                        squares(HEADS_AT.index(s - 1))
                    if s % TB == 0:
                        evacuate(PAIR // TB * it + s // TB - 1, (s // TB - 1) % 2)
                    if last and s == PAIR:
                        roots(0, CHUNKS - 1)

            def squares(c):
                act.wait_ge(heads_ps, c + 1)
                if c >= 2:
                    act.wait_ge(ss_done, c - 1)
                nc.scalar.activation(sq[c % 2], ps[:, HEADS_BANK[c], :], ACT.Square).then_inc(sq_done, 1)

            def roots(c, end):
                act.wait_ge(ss_done, end)
                nc.scalar.activation(sd[:, c:end, :], ss[:, c:end, :], ACT.Sqrt, scale=1.0 / DV,
                                     bias=epsc[:, 0:1]).then_inc(std_done, 1)

            def evacuate(a, th):
                act.wait_ge(e_free, 2 + TB * (a + 1))
                act.wait_ge(u_free, a + 1)
                nc.scalar.activation(A[:, th, :], ps[:, B_PV, :], ACT.Copy).then_inc(a_out, 1)

            exps(0, 0)
            with act.Fori(0, PAIRS - 1) as it:
                turn(it, False)
            turn(PAIRS - 1, True)

            squares(CHUNKS - 1)
            roots(CHUNKS - 1, CHUNKS)
            for k, c in enumerate(TAIL_ORDER):
                act.wait_ge(o_ps, k + 1)
                nc.scalar.activation(RES[:, c * FC:(c + 1) * FC, :].rearrange("p n d -> p (n d)"), ps[:, O_BANK[c], :],
                                     ACT.Copy).then_inc(o_done, 1)

        @block.vector
        def _(dve):
            chain = [0]

            def link(ins):
                chain[0] += 1
                ins.then_inc(dch, 1)
                dve.wait_ge(dch, chain[0])

            nc.vector.memset(Q[:, 1, 0:BANK].bitcast(F32), 0.0).then_inc(zeros_done, 1)
            for b in range(BATCH):
                dve.wait_ge(x_in[b], 16)
                for n in range(b * TB, (b + 1) * TB):
                    last = nc.vector.bn_stats(stats[:, n, :], X[:, n, :])
                link(last)
                for n in range(b * TB, (b + 1) * TB):
                    nc.vector.bn_aggr(mv[:, n, :], stats[:, n, :]).then_inc(mv_done, 1)
            for b in range(BATCH):
                r, v, t = rstd[:, b * TB:(b + 1) * TB], lnt[:, 0, :], lnt[:, 1, :]
                dve.wait_ge(sd_done, b + 1)
                link(nc.vector.reciprocal(r, r))
                link(nc.vector.tensor_scalar(v, mv[:, b * TB:(b + 1) * TB, 1], EPS, -0.5, ALU.add, ALU.mult))
                link(nc.vector.tensor_tensor(t, r, r, ALU.mult))
                link(nc.vector.tensor_tensor(t, t, v, ALU.mult))
                link(nc.vector.scalar_tensor_tensor(r, t, 1.5, r, ALU.add, ALU.mult))
                nc.vector.scalar_tensor_tensor(shift[:, b * TB:(b + 1) * TB], mv[:, b * TB:(b + 1) * TB, 0], -1.0, r,
                                               ALU.mult, ALU.mult).then_inc(shift_done, 1)
                for n in range(b * TB, b * TB + FC):
                    nc.vector.tensor_scalar(XN[:, n, :], X[:, n, :], mv[:, n, 0:1], rstd[:, n:n + 1],
                                            ALU.subtract, ALU.mult).then_inc(xn_done, 1)
            for c in range(CHUNKS):
                dve.wait_ge(xh_done, c + 1)
                nc.vector.tensor_tensor(xnL[:, c * BANK:(c + 1) * BANK], ps[:, c, :],
                                        xnH[:, c * BANK:(c + 1) * BANK], ALU.subtract).then_inc(xl_done, 1)
                nc.vector.tensor_reduce(sums[:, c:c + 1], ps[:, c, :], AX.X, ALU.add).then_inc(sums_done, 1)
            dve.wait_ge(s_in, 16 * 6)
            nc.vector.tensor_tensor(lam_p[:], lam_in[:, 0:4:2], lam_in[:, 1:4:2], ALU.mult).then_inc(lam_prod, 1)
            dve.wait_ge(sums_done, CHUNKS)
            link(nc.vector.tensor_tensor(pooled[:], sums[:, 0:CHUNKS:CB], sums[:, 1:CHUNKS:CB], ALU.add))
            nc.vector.tensor_scalar(pooled[:], pooled[:], 1.0 / SEQ, None, ALU.mult).then_inc(pool_done, 1)

            dve.wait_ge(tab_in, 16)

            def rotary(m):
                kind, c = (m // CB) % 2, m % CB
                for r in range(2):
                    k = 2 * m + r
                    dve.wait_ge(proj_done, k + 1)
                    if m >= ROT_BUFS:
                        dve.wait_ge(rope_done, m - ROT_BUFS + 1)
                    nc.vector.tensor_tensor(rot[:, m % ROT_BUFS, r, :], ps[:, proj_bank(k), :],
                                            tab[:, 2 * kind + r, c * BANK:(c + 1) * BANK],
                                            ALU.mult).then_inc(rot_done, 1)

            for m in range(2):
                rotary(m)

            def wb_zone(e, e2, par, b, first=False):
                if b == 0:
                    dve.wait_ge(raw_in[par], 32 * (e2 + 1))
                    if not first:
                        dve.wait_ge(hs_free, H_BUFS + UZ * (e - 1))
                w = wbc[:, bass.ds(b * ZONES + e, 1)]
                nc.vector.tensor_scalar(wbH[:, par, b, :], wb_raw[:, par, :], w, None, ALU.mult).then_inc(wbh_done, 1)
                dve.wait_ge(wbh_done, BATCH * e + b + 1)
                nc.vector.scalar_tensor_tensor(wbL[:, par, b, :], wb_raw[:, par, :], w, wbH[:, par, b, :],
                                               ALU.mult, ALU.subtract).then_inc(wb_split, 1)

            dve.wait_ge(logit_ps, 1)
            nc.vector.tensor_reduce(rt[:, 0:1], ps[0:BATCH, 7, 16:16 + ZONES], AX.X, ALU.max,
                                    negate=True).then_inc(negl, 1)
            for m in range(2, 4):
                rotary(m)
            dve.wait_ge(expl, 1)
            e_, p_ = rt[:, 8:16], rt[:, 16:24]
            gt = rt[:, 64:128].rearrange("b (e j) -> b e j", j=ZONES)
            eq = rt[:, 128:192].rearrange("b (e j) -> b e j", j=ZONES)
            tri = cst[0:BATCH, C_TRI:C_TRI + 64].rearrange("b (e j) -> b e j", j=ZONES)
            pj = rt[:, 16:24].unsqueeze(1).broadcast_to([BATCH, ZONES, ZONES])
            pe_ = rt[:, 16:24].unsqueeze(2).broadcast_to([BATCH, ZONES, ZONES])
            link(nc.vector.tensor_reduce(rt[:, 1:2], e_, AX.X, ALU.add))
            link(nc.vector.reciprocal(rt[:, 2:3], rt[:, 1:2]))
            link(nc.vector.tensor_scalar(p_, e_, rt[:, 2:3], None, ALU.mult))
            link(nc.vector.tensor_tensor(gt, pj, pe_, ALU.is_gt))
            link(nc.vector.tensor_tensor(eq, pj, pe_, ALU.is_equal))
            link(nc.vector.tensor_tensor(eq, eq, tri, ALU.mult))
            link(nc.vector.tensor_tensor(gt, gt, eq, ALU.add))
            link(nc.vector.tensor_reduce(rt[:, 24:32], gt, AX.X, ALU.add))
            link(nc.vector.tensor_scalar(rt[:, 32:40], rt[:, 24:32], TOP_K - 0.5, None, ALU.is_lt))
            link(nc.vector.tensor_tensor(rt[:, 40:48], rt[:, 32:40], p_, ALU.mult))
            link(nc.vector.tensor_reduce(rt[:, 3:4], rt[:, 40:48], AX.X, ALU.add))
            link(nc.vector.reciprocal(rt[:, 4:5], rt[:, 3:4]))
            nc.vector.tensor_scalar(rt[:, 48:56], rt[:, 40:48], rt[:, 4:5], None, ALU.mult).then_inc(wsel, 1)
            rotary(4)
            dve.wait_ge(wb_ps, 1)
            nc.vector.tensor_copy(wbc[:], ps[:, 7, 64:64 + BATCH * ZONES]).then_inc(wbc_done, 1)
            dve.wait_ge(wbc_done, 1)
            for b in range(BATCH):
                wb_zone(0, 0, 0, b, True)
            for m in range(5, 8):
                rotary(m)
            def reduce_bank(slot, x, half, col, sh):
                dve.wait_ge(slot_made, slot + 1)
                nc.vector.tensor_reduce(part_max[:, half, col, sh:sh + 1], ps[:, ring_bank(x), :], AX.X,
                                        ALU.max).then_inc(slot_read, 1)

            def max_split(hx, half, slot, x):
                dve.wait_ge(slot_made, slot + 1)
                nc.vector.tensor_copy(maxH[:, half, :], ps[0:16, ring_bank(x), 0:P]).then_inc(maxh_done, 1)
                dve.wait_ge(maxh_done, hx + 1)
                nc.vector.tensor_tensor(maxL[:, half, :], ps[0:16, ring_bank(x), 0:P], maxH[:, half, :],
                                        ALU.subtract).then_inc(slot_read, 1)

            def max_unit(it, o, last):
                if last and 2 * PAIR * it + o >= ALL_UNITS:
                    return
                x, k, h = unit_slot(o), o % UG, o // (UG // 2)
                base = PAIR_SLOTS * it
                for sh in range(2):
                    reduce_bank(base + x + sh, x + sh, h % 2, k % GJ * FC + k // GJ % FC, sh)
                if o % (UG // 2) == UG // 2 - 1:
                    dve.wait_ge(slot_read, base + x + 2)
                    nc.vector.tensor_reduce(neg_max[:, h % 2, :], part_max[:, h % 2, :, :], AX.X, ALU.max,
                                            negate=True).then_inc(neg_done, 1)
                if o % (UG // 2) == 1 and h:
                    max_split(4 * it + h - 1, (h - 1) % 2, base + half_slot(h - 1), half_slot(h - 1))
                if last and 2 * PAIR * it + o == ALL_UNITS - 1:
                    max_split(2 * GROUPS - 1, 1, SLOTS - 1, SLOTS - 1)

            def residual(c):
                r = slice(c * FC, (c + 1) * FC)
                dve.wait_ge(zt_done, c + 1)
                nc.vector.tensor_tensor(RES[:, r, :].rearrange("p n d -> p (n d)"), ps[:, back_bank(c), :],
                                        X[:, r, :].rearrange("p n d -> p (n d)"),
                                        ALU.add).then_inc(res_done if c < CHUNKS - 1 else a_out, 1)

            def split_turn(it, lead, last):
                for s in range(2 * UZ):
                    n = 2 * UZ * it + s
                    dve.wait_ge(hh_done, n + 1)
                    nc.vector.tensor_tensor(hL[:, s % H_BUFS, :], h[:, s % 2, :], hH[:, s % H_BUFS, :],
                                            ALU.subtract).then_inc(split_done, 1)
                    if s in (FC, 2 * FC):
                        wb_zone(2 * it + 1, it, 1, s // FC - 1)
                    if s in (UZ + FC, UZ + 2 * FC) and not last:
                        wb_zone(2 * it + 2, it + 1, 0, (s - UZ) // FC - 1)
                    if lead and lead_unit(2 * UZ * last + s - 2) is not None:
                        max_unit(0, lead_unit(2 * UZ * last + s - 2), False)
                    if last and sum_chunk(s, 6) is not None:
                        residual(sum_chunk(s, 6))

            with dve.Fori(0, ZONES // 2 - 2) as it:
                split_turn(it, False, False)
            dve.wait_ge(lam_exp, 1)
            nl, ab, cc, c2, nlc = (lt[:, k:k + 1] for k in range(5))
            link(nc.vector.scalar_tensor_tensor(nl, lam_e[:, 1:2], LAMBDA_INIT, lam_e[:, 0:1],
                                                ALU.subtract, ALU.subtract))
            link(nc.vector.tensor_scalar(ab, nl, -1.0, None, ALU.mult))
            link(nc.vector.tensor_tensor(ab, ab, nl, ALU.max))
            link(nc.vector.tensor_scalar(ab, ab, 1.0, None, ALU.add))
            link(nc.vector.reciprocal(cc, ab))
            link(nc.vector.tensor_scalar(cc, cc, LAMBDA_RANGE, 1.0, ALU.mult, ALU.min))
            link(nc.vector.tensor_tensor(c2, cc, cc, ALU.mult))
            link(nc.vector.tensor_scalar(epsc[:], c2, EPS, SQRT_LEAST, ALU.mult, ALU.max))
            link(nc.vector.tensor_scalar(limit[:], c2, FLT_MAX, None, ALU.mult))
            link(nc.vector.tensor_tensor(nlc, nl, cc, ALU.mult))
            link(nc.vector.tensor_scalar(comb[:], cst[:, C_E0:C_E0 + 2 * QUAD], cc, None, ALU.mult))
            nc.vector.scalar_tensor_tensor(comb[:], cst[:, C_E1:C_E1 + 2 * QUAD], nlc, comb[:],
                                           ALU.mult, ALU.add).then_inc(comb_done, 1)
            split_turn(ZONES // 2 - 2, True, False)
            split_turn(ZONES // 2 - 1, True, True)
            for u in range(4 * UZ - 2, 4 * UZ):
                if lead_unit(u) is not None:
                    max_unit(0, lead_unit(u), False)
            for c in range(2, CHUNKS):
                residual(c)
            for v in range(LEAD, LEAD + 2 * BEHIND):
                max_unit(0, v, False)

            def query_rows(a, th, part):
                if part == 0:
                    dve.wait_ge(a_out, a + 2)
                if part < 2:
                    h = slice(part * BANK // 2, (part + 1) * BANK // 2)
                    nc.vector.transpose(AT[:, th, h], A[:, th, h]).then_inc(at_done, 1)
                else:
                    dve.wait_ge(at_done, 2 * a + 2)
                    nc.vector.reciprocal(rsum[:, th, :],
                                         AT[:, th, :].rearrange("p (k c) -> p k c", c=QUAD)[:, :, DV]).then_inc(rsum_done, 1)

            def normalise_last():
                a = 2 * GROUPS - 1
                dve.wait_ge(rsum_done, a + 1)
                nc.vector.tensor_tensor(U[:, a * HALF_U:].rearrange("p (k c) -> p k c", c=DV), products(1),
                                        rsum[:, 1, :].unsqueeze(2).broadcast_to([P, NB, DV]), ALU.mult).then_inc(u_free, 1)

            def square_sums(c):
                dve.wait_ge(sq_done, c + 1)
                nc.vector.tensor_reduce(ss[:, c, :], sq[c % 2].rearrange("p (n v) -> p n v", v=DV), AX.X,
                                        ALU.add).then_inc(ss_done, 1)

            def shares(c, end):
                last_one = int(end == CHUNKS)
                dve.wait_ge(std_done, last_one + 1)
                nc.vector.reciprocal(sd[:, c:end, :], sd[:, c:end, :]).then_inc(rcp_done, 1)
                dve.wait_ge(rcp_done, last_one + 1)
                nc.vector.scalar_tensor_tensor(sd[:, c:end, :], ss[:, c:end, :], limit[:, 0:1], sd[:, c:end, :],
                                               ALU.is_le, ALU.mult).then_inc(rms_done, 1)
                dve.wait_ge(rms_done, last_one + 1)

            def normalise(c, count):
                nc.vector.scalar_tensor_tensor(
                    X[:, c * FC:(c + 1) * FC, :].rearrange("p n (h v) -> p (n h) v", v=DV),
                    ps[:, HEADS_BANK[c], :].rearrange("p (n v) -> p n v", v=DV), 1.0 - LAMBDA_INIT,
                    sd[:, c, :].unsqueeze(2).broadcast_to([P, QUAD, DV]), ALU.mult, ALU.mult).then_inc(an_done, 1)
                dve.wait_ge(an_done, count)
                nc.vector.transpose(zT[:, c * BANK:(c + 1) * BANK],
                                    X[:, c * FC:(c + 1) * FC, :].rearrange("p n d -> p (n d)")).then_inc(ant_done, 1)

            def turn(it, last):
                for s in range(PAIR):
                    for u in range(2):
                        max_unit(it, LEAD + 2 * BEHIND + 2 * s + u, last)
                    half = s // TB
                    if last and s == HEADS_AT[0] - BEHIND:
                        square_sums(0)
                        square_sums(1)
                    if last and s == PAIR - BEHIND:
                        square_sums(2)
                    if 0 <= s % TB - (TB - BEHIND) < 3:
                        query_rows(PAIR // TB * it + half, half % 2, s % TB - (TB - BEHIND))

            with dve.Fori(0, PAIRS - 1) as it:
                turn(it, False)
            turn(PAIRS - 1, True)

            normalise_last()
            shares(0, CHUNKS - 1)
            normalise(0, 1)
            normalise(1, 2)
            square_sums(3)
            shares(CHUNKS - 1, CHUNKS)
            normalise(3, 3)
            normalise(2, 4)

        @block.tensor
        def _(pe):
            mm = nc.tensor.matmul
            def keep_warm(n):
                for _ in range(n):
                    mm(ps[:, 7, :], Q[:, 1, 0:P], Q[:, 1, 0:BANK], start=True, stop=True)

            pe.wait_ge(zeros_done, 1)
            keep_warm(WARM_UP)
            pe.wait_ge(c_in, 16)
            for c in range(CHUNKS):
                pe.wait_ge(xa_done if c % CB else xn_done, FC * (c // CB + 1))
                for k in range(FC):
                    last = nc.tensor.transpose(ps[:, c, k * P:(k + 1) * P], XN[:, c * FC + k, :], ident)
                last.then_inc(xt_done, 1)
                if c == CB - 1:
                    keep_warm(5)
            def three(o, lh, ll, rh, rl, start, stop):
                mm(o, lh, rh, start=start, stop=False)
                mm(o, lh, rl, start=False, stop=False)
                return mm(o, ll, rh, start=False, stop=stop)

            pe.wait_ge(w_split, 1)

            def project(k):
                m, r = k // 2, k % 2
                kind, c = (m // CB) % 2, (m // (2 * CB)) * CB + m % CB
                pe.wait_ge(xl_done, c + 1)
                if k >= 3:
                    pe.wait_ge(rot_done, k - 2 + (k >= 14))
                t = slice(c * BANK, (c + 1) * BANK)
                three(ps[:, proj_bank(k), :], wH[:, 2 * kind + r, :], wL[:, 2 * kind + r, :], xnH[:, t], xnL[:, t],
                      True, True).then_inc(proj_done, 1)

            def values(c):
                pe.wait_ge(sums_done, c + 1)
                for k in range(FC):
                    t = slice((c * FC + k) * P, (c * FC + k + 1) * P)
                    last = three(ps[:, c, k * P:(k + 1) * P], xnH[:, t], xnL[:, t], wH[:, 4, :], wL[:, 4, :], True, True)
                last.then_inc(v_done, 1)

            project(0)
            project(1)
            values(0)
            project(2)
            values(1)
            pe.wait_ge(pool_done, 1)
            pe.wait_ge(s_in, 16 * 6)
            mm(ps[0:ROUTER, 7, 8:8 + BATCH], w1_in[:], pooled[:], start=True, stop=True).then_inc(hid_ps, 1)
            project(3)
            pe.wait_ge(lam_prod, 1)
            pe.wait_ge(hid_sb, 1)
            mm(ps[:, 7, 32:34], cst[0:DQ, C_ONE:C_ONE + P], lam_p[:], start=True, stop=True).then_inc(lam_ps, 1)
            pe.wait_ge(lam_exp, 1)
            mm(ps[0:BATCH, 7, 16:16 + ZONES], hid[:], w2_in[:], start=True, stop=False)
            mm(ps[0:BATCH, 7, 16:16 + ZONES], cst[0:1, C_ONE:C_ONE + BATCH], b2_in[:], start=False,
               stop=True).then_inc(logit_ps, 1)
            for k in range(4, 10):
                project(k)
                if k in (7, 9):
                    values(k // 2 - 1)
            project(10)
            pe.wait_ge(wsel, 1)
            for b in range(BATCH):
                last = mm(ps[:, 7, 64 + b * ZONES:64 + (b + 1) * ZONES], cst[0:BATCH, C_SEL + b * P:C_SEL + (b + 1) * P],
                          rt[:, 48:56], start=True, stop=True)
            last.then_inc(wb_ps, 1)
            project(11)
            project(12)
            pe.wait_ge(v_out, CHUNKS)
            pe.wait_ge(id_done, 1)
            for c in range(CHUNKS):
                t = slice(c * BANK, (c + 1) * BANK)
                mm(ps[:, c, :], identR[:], xnH[:, t], start=True, stop=False, skip_group_check=True)
                last = mm(ps[:, c, :], identR[:], xnL[:, t], start=False, stop=False, skip_group_check=True)
            last.then_inc(hs_free, H_BUFS)

            def first(s, par):
                c, f = s % UZ // FC, s % FC
                t = slice(c * BANK, (c + 1) * BANK)
                f = slice(f * P, (f + 1) * P)
                three(ps[:, 6 + s % 2, :], waH[:, par, f], waL[:, par, f], xnH[:, t], xnL[:, t],
                      True, True).then_inc(g1_done, 1)

            def second(s, par, end):
                c, f, buf = s % UZ // FC, s % FC, s % H_BUFS
                fs = slice(f * P, (f + 1) * P)
                for i, (l, r) in enumerate(((wbH, hH), (wbH, hL), (wbL, hH))):
                    last = mm(ps[:, c, :], l[:, par, c // CB, fs], r[:, buf, :], start=False,
                              stop=end and f == FC - 1 and i == 2, skip_group_check=True)
                last.then_inc(hs_free, 1)

            pe.wait_ge(wa_split, 1)
            project(13)
            pe.wait_ge(rot_done, 12)
            first(0, 0)
            for k in range(14, 16):
                project(k)
            pe.wait_ge(wbc_done, 1)
            first(1, 0)
            pe.wait_ge(gelu_done, 1)
            first(2, 0)

            def ffn_turn(it, lead, last):
                for s in range(2 * UZ):
                    n, a = 2 * UZ * it + s, s + H_LEAD
                    if not (last and a >= 2 * UZ):
                        if a % UZ == 0:
                            pe.wait_ge(wa_split, 2 * it + a // UZ + 1)
                        pe.wait_ge(gelu_done, n + H_LEAD - 1)
                        first(a % (2 * UZ), a // UZ % 2)
                    if s % UZ == 0:
                        pe.wait_ge(wb_split, BATCH * (2 * it + s // UZ + 1))
                    pe.wait_ge(split_done, n + 1)
                    second(s, s // UZ, last and s >= UZ)
                    if lead and lead_unit(2 * UZ * last + s) is not None:
                        for sh in range(2):
                            max_slot(0, lead_unit(2 * UZ * last + s), sh, False)
                    if last and sum_chunk(s, 3) is not None:
                        back(sum_chunk(s, 3))

            def back(c):
                pe.wait_ge(z_out, c + 1)
                for k in range(FC):
                    last = nc.tensor.transpose(ps[:, back_bank(c), k * P:(k + 1) * P],
                                               zT[:, (c * FC + k) * P:(c * FC + k + 1) * P], ident)
                last.then_inc(zt_done, 1)

            def half_transpose(hx, half, slot, x):
                pe.wait_ge(neg_done, hx + 1)
                pe.wait_ge(slot_read, slot - (1 if x < LEAD_SLOTS else 2))
                nc.tensor.transpose(ps[0:16, ring_bank(x), 0:P], neg_max[:, half, :], ident).then_inc(slot_made, 1)

            def max_slot(it, o, sh, last):
                if last and 2 * PAIR * it + o >= ALL_UNITS:
                    return
                x, k, g, h = unit_slot(o), o % UG, o // UG, o // (UG // 2)
                base = PAIR_SLOTS * it
                if k == 0 and sh == 0:
                    pe.wait_ge(kq_in, 16 * (GJ + 1) * (2 * it + g + 1))
                back_to = 1 if x < LEAD_SLOTS else 2
                if x + sh > back_to:
                    pe.wait_ge(slot_read, base + x + sh - back_to)
                mm(ps[:, ring_bank(x + sh), :], Q[:, g % 2, k // GJ * P:(k // GJ + 1) * P],
                   K[:, g % 2, k % GJ, sh * BANK:(sh + 1) * BANK], start=True, stop=True).then_inc(slot_made, 1)
                if o % (UG // 2) == 1 and h and sh:
                    half_transpose(4 * it + h - 1, (h - 1) % 2, base + half_slot(h - 1), half_slot(h - 1))

            def heads_sum(c):
                b, th = c // CB, c % CB
                if c == 0:
                    pe.wait_ge(comb_done, 1)
                    pe.wait_ge(slot_read, SLOTS)
                for g in range(GB):
                    a, rows = 2 * (b * GB + g) + th, 2 * QUAD * (g % 2)
                    pe.wait_ge(u_free, 2 + a + 1)
                    o = ps[rows:rows + 2 * QUAD, HEADS_BANK[c], :].rearrange("p (k r c) -> p k r c", r=2, c=DV)
                    last = mm(o[:, :, g // 2, :], comb[:], U[:, a * HALF_U:(a + 1) * HALF_U], start=True, stop=True)
                last.then_inc(heads_ps, 1)

            def scores(s, par, jj):
                th, st = s // TB, s % TB
                for j in (2 * jj, 2 * jj + 1):
                    last = mm(ps[:, j, :], K[:, par, j, st * P:(st + 1) * P], Q[:, par, th * BANK:(th + 1) * BANK],
                              start=True, stop=True)
                last.then_inc(st_done, 1)

            def probs_v(s, par):
                st = s % TB
                for j in range(GJ):
                    last = mm(ps[QUAD * j:QUAD * (j + 1), B_PV, :], Vg[:, par, st, j // 2, :], E[:, s % 2, j, :],
                              start=(st == 0), stop=(st == TB - 1), skip_group_check=True)
                last.then_inc(e_free, 1)

            with pe.Fori(0, ZONES // 2 - 2) as it:
                ffn_turn(it, False, False)
            ffn_turn(ZONES // 2 - 2, True, False)
            ffn_turn(ZONES // 2 - 1, True, True)
            pe.wait_ge(qmax_in, 32)
            pe.wait_ge(res_done, 2)
            pe.sem_inc(e_free, 2)
            scores(0, 0, 0)
            pe.wait_ge(z_out, CHUNKS)
            pe.wait_ge(res_done, CHUNKS - 1)
            scores(0, 0, 1)
            pe.wait_ge(gelu_done, UNITS)
            back(CHUNKS - 1)
            pe.wait_ge(slot_read, LEAD_SLOTS)

            def turn(it, last):
                for s in range(PAIR):
                    n, p = PAIR * it + s, s // STEPS
                    nxt = s + 1
                    ahead = not (last and nxt == PAIR)
                    o = LEAD + 2 * s
                    for jj in range(2):
                        max_slot(it, o, jj, last)
                        if ahead:
                            if jj == 0 and nxt % TB == 0:
                                pe.wait_ge(qmax_in, 32 * (4 * it + nxt // TB + 1))
                            pe.wait_ge(exp_done, 2 * n + jj + 1)
                            scores(nxt % STEPS, (nxt // STEPS) % 2, jj)
                    for sh in range(2):
                        max_slot(it, o + 1, sh, last)
                    if last and 2 * PAIR * it + o == ALL_UNITS:
                        half_transpose(2 * GROUPS - 1, 1, SLOTS - 1, SLOTS - 1)
                    if last and s in HEADS_AT:
                        heads_sum(HEADS_AT.index(s))
                    if s % STEPS == 0:
                        pe.wait_ge(vg_done, 2 * it + p + 1)
                    if s % TB == 0:
                        pe.wait_ge(a_out, PAIR // TB * it + s // TB + 1)
                    pe.wait_ge(exp_done, 2 * n + 2)
                    probs_v(s % STEPS, p)

            with pe.Fori(0, PAIRS - 1) as it:
                turn(it, False)
            turn(PAIRS - 1, True)

            def residual(c):
                mm(ps[:, O_BANK[c], :], ident, RES[:, c * FC:(c + 1) * FC, :].rearrange("p n d -> p (n d)"),
                   start=True, stop=False, skip_group_check=True)

            def product(c, count):
                pe.wait_ge(ant_done, count)
                for k in range(FC):
                    last = mm(ps[:, O_BANK[c], k * P:(k + 1) * P], zT[:, (c * FC + k) * P:(c * FC + k + 1) * P],
                              wo_in[:], start=False, stop=k == FC - 1, skip_group_check=True)
                last.then_inc(o_ps, 1)

            pe.wait_ge(exp_done, 2 * ALL_STEPS)
            for c in range(2):
                residual(c)
            heads_sum(3)
            residual(2)
            pe.wait_ge(a_out, 2 * GROUPS + 1)
            residual(3)
            for k, c in enumerate(TAIL_ORDER):
                product(c, k + 1)


def feature_order():
    e = np.arange(P).reshape(2, 2, 2, DV)
    return e.transpose(1, 2, 0, 3).reshape(P)


def shape_constants():
    c = np.zeros((P, C_END), np.float32)
    r = np.arange(P)
    c[:, C_ID:C_ID + P] = np.eye(P)
    for j in range(GJ):
        for i in range(QUAD):
            c[QUAD * j + i, (C_E0 if j % 2 == 0 else C_E1) + (j // 2) * QUAD + i] = 1
    for b in range(BATCH):
        c[b, C_SEL + b * P:C_SEL + (b + 1) * P] = 1
    c[0:BATCH, C_TRI:C_TRI + 64] = (np.arange(ZONES)[None, :] < np.arange(ZONES)[:, None]).reshape(-1)
    c[:, C_ONE:] = 1
    inv_freq = np.float32(1) / np.float32(10000) ** (np.arange(0, DQ, 2, dtype=np.float32) / np.float32(DQ))
    pos = np.arange(SEQ, dtype=np.float32)
    freqs = np.repeat(pos[:, None] * inv_freq[None, :], 2, axis=-1).astype(np.float64)
    sv = (np.arange(0, DQ, 2, dtype=np.float32) + np.float32(0.4 * DQ)) / np.float32(1.4 * DQ)
    scale = sv[None, :].astype(np.float64) ** ((pos - SEQ // 2) / 512.0)[:, None]
    scale = np.concatenate([scale, scale], axis=-1)
    sign = np.where(np.arange(DQ) % 2 == 0, -1.0, 1.0)[None, :]
    q = scale * DQ ** -0.5
    t = np.stack([np.cos(freqs) * q, np.sin(freqs) * sign * q, np.cos(freqs) / scale, np.sin(freqs) * sign / scale])
    t = np.tile(t.transpose(2, 0, 1), (SUBHEADS, 1, 1)).astype(np.float32)
    return c, np.ascontiguousarray(t)


def kernel(**inputs):
    import concourse.bacc as bacc
    from concourse.bass_utils import run_bass_kernel_spmd

    g = {k: np.asarray(v) for k, v in inputs.items()}
    consts, tables = shape_constants()
    swap = np.arange(P) ^ 1
    wq, wk, wv = g["L0_attn_Wq"], g["L0_attn_Wk"], g["L0_attn_Wv"]
    arrays = {
        "x": g["L0_attn_x"].reshape(TOKENS, P),
        "wqkv": np.stack([wq.T, wq[swap].T, wk.T, wk[swap].T, wv.T], axis=1),
        "wo": g["L0_attn_Wo"].T[feature_order()],
        "lam": np.stack([g[f"L0_attn_lambda_{n}"] for n in ("q1", "k1", "q2", "k2")], axis=1),
        "w1": g["L0_ffn_W1"],
        "b1": g["L0_ffn_b1"].reshape(ROUTER, 1),
        "w2": g["L0_ffn_W2"],
        "b2": g["L0_ffn_b2"].reshape(1, ZONES),
        "wa": g["L0_ffn_Wa"],
        "wb": g["L0_ffn_Wb"].reshape(ZONES, FC, P, P).transpose(0, 2, 1, 3).reshape(ZONES, P, FF),
        "consts": consts,
        "tables": tables,
    }
    arrays = {f"in_{k}": np.ascontiguousarray(v) for k, v in arrays.items()}
    nc = bacc.Bacc("TRN2", target_bir_lowering=False, num_devices=1)
    args = [nc.dram_tensor(k, v.shape, mybir.dt.from_np(v.dtype), kind="ExternalInput").ap() for k, v in arrays.items()]
    out = nc.dram_tensor("out", (TOKENS, P), F32, kind="ExternalOutput").ap()
    build(nc, *args, out)
    r = run_bass_kernel_spmd(nc, [arrays], core_ids=[0])
    return r.results[0]["out"].reshape(BATCH, SEQ, P)
```
